# Optimizing a Trainium2 kernel written in Bass

```python
import numpy as np
import jax
import jax.numpy as jnp

def _softmax(x, axis=-1):
    return jax.nn.softmax(x, axis=axis)

def _gelu(x):
    return jax.nn.gelu(x, approximate=True)

def _silu(x):
    return jax.nn.silu(x)

def _sigmoid(x):
    return jax.nn.sigmoid(x)

def _layernorm(x, axis=-1, eps=1e-05):
    m = jnp.mean(x, axis=axis, keepdims=True)
    v = jnp.var(x, axis=axis, keepdims=True)
    return (x - m) / jnp.sqrt(v + eps)

def _scatter_add(tgt, idx, src, axis=0):
    return tgt.at[idx].add(src)

def _segment_sum(src, seg, n):
    return jax.ops.segment_sum(src, seg, n)
kernel_name = 'mk_prb_d1_jaxref_r4_0fa56d'

def setup_inputs(seed: int=0):
    np.random.seed(seed)
    _w = jnp.asarray

    def _L0_attn_setup():
        import jax, jax.numpy as jnp
        import numpy as np
        HIDDEN = 512
        N_HEADS = 32
        HEAD_DIM = HIDDEN // N_HEADS
        SEQ = 512
        BATCH = 1
        CHUNK = 64
        TOPK = 4
        THETA = 10000.0
        EPS = 1e-06
        NEG = jnp.float32(-1e+30)

        def _rope(t):
            D = t.shape[-1]
            pos = jnp.arange(t.shape[1], dtype=jnp.float32)
            inv_freq = 1.0 / THETA ** (jnp.arange(0, D, 2, dtype=jnp.float32) / D)
            freqs = pos[:, None] * inv_freq[None, :]
            cos = jnp.cos(freqs)[None, :, None, :]
            sin = jnp.sin(freqs)[None, :, None, :]
            t1, t2 = (t[..., :D // 2], t[..., D // 2:])
            return jnp.concatenate([t1 * cos - t2 * sin, t1 * sin + t2 * cos], axis=-1)
        key = jax.random.key(seed)
        ks = jax.random.split(key, 8)
        s = 0.02
        return {'hidden_states': jax.random.normal(ks[0], (BATCH, SEQ, HIDDEN), jnp.float32), 'Wq': jax.random.normal(ks[1], (HIDDEN, HIDDEN), jnp.float32) * s, 'Wk': jax.random.normal(ks[2], (HIDDEN, HIDDEN), jnp.float32) * s, 'Wv': jax.random.normal(ks[3], (HIDDEN, HIDDEN), jnp.float32) * s, 'Wo': jax.random.normal(ks[4], (HIDDEN, HIDDEN), jnp.float32) * s, 'Wg1': jax.random.normal(ks[5], (HEAD_DIM, HIDDEN), jnp.float32) * s, 'Wg2': jax.random.normal(ks[6], (HIDDEN, HEAD_DIM), jnp.float32) * s, 'o_norm_weight': jnp.ones((HEAD_DIM,), jnp.float32)}
    _L0_attn_in = _L0_attn_setup()

    def _L0_ffn_setup():
        import jax, jax.numpy as jnp
        import numpy as np
        RANK = 64
        SCALING = 1.0 / RANK
        TEMPERATURE = 1.0
        key = jax.random.key(seed)
        k_x, k_a, k_b, k_w = jax.random.split(key, 4)
        B_, S, D = (4, 512, 512)
        E, R, O = (8, RANK, 512)
        x = jax.random.normal(k_x, (B_, S, D), dtype=jnp.float32)
        A = jax.random.normal(k_a, (E, R, D), dtype=jnp.float32) * (1.0 / np.sqrt(D))
        Bw = jax.random.normal(k_b, (E, O, R), dtype=jnp.float32) * 0.02
        Wr = jax.random.normal(k_w, (E, D), dtype=jnp.float32) * (1.0 / np.sqrt(D))
        br = jnp.zeros((E,), dtype=jnp.float32)
        return {'x': x, 'A': A, 'B': Bw, 'Wr': Wr, 'br': br}
    _L0_ffn_in = _L0_ffn_setup()
    _d = {'L0_attn_hidden_states': _L0_attn_in['hidden_states'], 'L0_attn_Wq': _L0_attn_in['Wq'], 'L0_attn_Wk': _L0_attn_in['Wk'], 'L0_attn_Wv': _L0_attn_in['Wv'], 'L0_attn_Wo': _L0_attn_in['Wo'], 'L0_attn_Wg1': _L0_attn_in['Wg1'], 'L0_attn_Wg2': _L0_attn_in['Wg2'], 'L0_attn_o_norm_weight': _L0_attn_in['o_norm_weight'], 'L0_ffn_A': _L0_ffn_in['A'], 'L0_ffn_B': _L0_ffn_in['B'], 'L0_ffn_Wr': _L0_ffn_in['Wr'], 'L0_ffn_br': _L0_ffn_in['br']}
    _x0 = _d['L0_attn_hidden_states']
    _d['L0_attn_hidden_states'] = jax.random.normal(jax.random.fold_in(jax.random.key(seed), 1), (1, 2048, 512), dtype=_x0.dtype)
    del _x0
    return _d

def reference(L0_attn_hidden_states, L0_attn_Wq, L0_attn_Wk, L0_attn_Wv, L0_attn_Wo, L0_attn_Wg1, L0_attn_Wg2, L0_attn_o_norm_weight, L0_ffn_A, L0_ffn_B, L0_ffn_Wr, L0_ffn_br):

    def _L0_attn_ref(hidden_states, Wq, Wk, Wv, Wo, Wg1, Wg2, o_norm_weight):
        import jax, jax.numpy as jnp
        import numpy as np
        HIDDEN = 512
        N_HEADS = 32
        HEAD_DIM = HIDDEN // N_HEADS
        SEQ = 512
        BATCH = 1
        CHUNK = 64
        TOPK = 4
        THETA = 10000.0
        EPS = 1e-06
        NEG = jnp.float32(-1e+30)

        def _rope(t):
            D = t.shape[-1]
            pos = jnp.arange(t.shape[1], dtype=jnp.float32)
            inv_freq = 1.0 / THETA ** (jnp.arange(0, D, 2, dtype=jnp.float32) / D)
            freqs = pos[:, None] * inv_freq[None, :]
            cos = jnp.cos(freqs)[None, :, None, :]
            sin = jnp.sin(freqs)[None, :, None, :]
            t1, t2 = (t[..., :D // 2], t[..., D // 2:])
            return jnp.concatenate([t1 * cos - t2 * sin, t1 * sin + t2 * cos], axis=-1)
        B, S, _ = hidden_states.shape
        H, D, C = (N_HEADS, HEAD_DIM, CHUNK)
        NC = S // C
        q = (hidden_states @ Wq.T).reshape(B, S, H, D)
        k = (hidden_states @ Wk.T).reshape(B, S, H, D)
        v = (hidden_states @ Wv.T).reshape(B, S, H, D)
        q, k = (_rope(q), _rope(k))
        kmean = k.reshape(B, NC, C, H, D).mean(axis=2)
        gate = jnp.einsum('bshd,bnhd->bhsn', q, kmean)
        pos = jnp.arange(S)
        q_chunk = pos // C
        chunk_ids = jnp.arange(NC)
        future = chunk_ids[None, :] > q_chunk[:, None]
        self_blk = chunk_ids[None, :] == q_chunk[:, None]
        gate = jnp.where(future[None, None], NEG, gate)
        gate = jnp.where(self_blk[None, None], -NEG, gate)
        _, topk_idx = jax.lax.top_k(gate, TOPK)
        sel = jax.nn.one_hot(topk_idx, NC, dtype=jnp.bool_).any(axis=-2)
        allowed = jnp.take(sel, q_chunk, axis=-1)
        causal = pos[None, :] <= pos[:, None]
        allowed = allowed & causal[None, None]
        scale = 1.0 / np.sqrt(D)
        scores = jnp.einsum('bshd,bthd->bhst', q, k) * scale
        scores = jnp.where(allowed, scores, NEG)
        p = jax.nn.softmax(scores, axis=-1)
        o = jnp.einsum('bhst,bthd->bshd', p, v)
        g = (hidden_states @ Wg1.T @ Wg2.T).reshape(B, S, H, D)
        rms = jax.lax.rsqrt(jnp.mean(o * o, axis=-1, keepdims=True) + EPS)
        o = o * rms * o_norm_weight * jax.nn.sigmoid(g)
        return o.reshape(B, S, H * D) @ Wo.T

    def _L0_ffn_ref(x, A, B, Wr, br):
        import jax, jax.numpy as jnp
        import numpy as np
        RANK = 64
        SCALING = 1.0 / RANK
        TEMPERATURE = 1.0
        batch, seq, d = x.shape
        E, out_dim = (B.shape[0], B.shape[1])
        x_flat = x.reshape(-1, d)
        logits = (x_flat @ Wr.T + br) / TEMPERATURE
        probs = jax.nn.softmax(logits, axis=-1)
        expert_idx = jnp.argmax(probs, axis=-1)
        expert_weight = jnp.max(probs, axis=-1)
        h = jnp.einsum('nd,erd->ner', x_flat, A)
        y = jnp.einsum('ner,eor->neo', h, B) * SCALING
        sel = jnp.take_along_axis(y, expert_idx[:, None, None], axis=1)[:, 0, :]
        out_flat = sel * expert_weight[:, None]
        return out_flat.reshape(batch, seq, out_dim)
    x = L0_attn_hidden_states
    xn = _layernorm(x, axis=-1)
    x = x + _L0_attn_ref(xn, L0_attn_Wq, L0_attn_Wk, L0_attn_Wv, L0_attn_Wo, L0_attn_Wg1, L0_attn_Wg2, L0_attn_o_norm_weight) + _L0_ffn_ref(xn, L0_ffn_A, L0_ffn_B, L0_ffn_Wr, L0_ffn_br)
    return x

_drawn_inputs = setup_inputs


def setup_inputs(seed=0):
    import zlib

    import numpy as np

    out = dict(_drawn_inputs(seed))
    spreads = {'L0_attn_o_norm_weight': (1.0, 0.2), 'L0_ffn_br': (0.0, 0.8)}
    factors = {'L0_attn_Wg1': 8.0, 'L0_attn_Wg2': 8.0, 'L0_ffn_A': 8.0, 'L0_ffn_B': 8.0, 'L0_ffn_Wr': 8.0}
    for name, (base, spread) in spreads.items():
        noise = np.random.default_rng([zlib.crc32(name.encode()), seed]).standard_normal(out[name].shape)
        drawn = base * np.exp(spread * noise) if base else spread * noise
        out[name] = jnp.asarray(drawn.astype(out[name].dtype))
    for name, factor in factors.items():
        out[name] = (out[name] * factor).astype(out[name].dtype)
    return out
```

```python
from contextlib import ExitStack

import numpy as np

import concourse.bass as bass
from concourse import mybir

P = 128
S = 2048
D = 512
NH = 32
HD = 16
HH = HD // 2
CH = 64
NC_ = S // CH
TOPK = 4
NE = 8
RANK = 64
NEG = -1e30
MASK = -float(2 ** 46)
KT = D // P
QT = S // P
BW = 512
NB = S // BW
VW = HD + 1
KC = S + NC_
SENT = 3.0e38
HIT = 2.0e38
RMS_EPS = 1e-6
LN_EPS = 1e-5
NPART = 3
RING = 4

F32 = mybir.dt.float32
BF16 = mybir.dt.bfloat16
ALU = mybir.AluOpType
ACT = mybir.ActivationFunctionType
AX = mybir.AxisListType

PIECES = [(i, p) for i in range(QT) for p in range(i // 4 + 1)]
TILES = [(b, j) for b in range(NB) for j in range(4 * b + 4)]
NP_ = len(PIECES)
NG = NP_ // 4
assert len(TILES) == NP_ and NP_ % 8 == 0
LAST_GROUP = {sum(1 for t in TILES if t[0] <= b) // 4 - 1: b for b in range(NB)}
BANK1 = [n % 3 for n in range(NP_)]
BANK1[NP_ - 1] = 1
LEAD = 2


def bank1_before(n):
    k = 1
    while BANK1[(n - k) % NP_] != BANK1[n]:
        k += 1
    return k


def misc_base(h, hi):
    if hi is None or 1 <= hi <= 30:
        return 11 + 5 * (h - 1)
    return {-2: 0, -1: 3, 0: 7, 31: 11 + 5 * 29 + 2, 32: 11 + 5 * 29 + 3}[hi]


def misc_slot(what, hi):
    order = []
    if hi is None or hi + 2 < NH:
        order.append("gates")
    if hi is None or 1 <= hi:
        order.append("merge")
    if hi is None or hi + 2 < NH:
        order += ["mask0", "mask1"]
    if hi is None or 0 <= hi + 1 < NH:
        order.append("max")
    return order.index(what)


def valid(h):
    return not isinstance(h, int) or 0 <= h < NH


def wait(eng, sem, value):
    if isinstance(value, int) and value <= 0:
        return
    eng.wait_ge(sem, value)


def all_steps(eng, step):
    def peeled(h):
        step(h, h % RING, h // RING, h)

    for h in range(-2, 3):
        peeled(h)
    with eng.Fori(0, 6) as it:
        for u in range(3, 3 + RING):
            step(it * RING + u, u % RING, it + u // RING, None)
    for h in range(27, NH + 1):
        peeled(h)


def build(nc, x, wqkv, wlr, wg2, wo, wa, wb, onorm, br, rope, krows, cbias, identf, identb, tri,
          sel, hmean, out):
    q_parts = nc.dram_tensor("q_parts", (NH, NPART, HD, S), BF16, kind="Internal").ap()
    k_parts = nc.dram_tensor("k_parts", (NH, NPART, HD, KC), BF16, kind="Internal").ap()
    u_dram = nc.dram_tensor("u_dram", (NH, P, BW), F32, kind="Internal").ap()
    ew_dram = nc.dram_tensor("ew_dram", (NE, S), F32, kind="Internal").ap()
    xr = x.rearrange("a (n p) d -> p (a n) d", p=P)
    outr = out.rearrange("a (n p) d -> p (a n) d", p=P)

    with ExitStack() as ctx:
        def sb(name, shape, dt):
            return ctx.enter_context(nc.sbuf_tensor(name, shape, dt))

        def sem(name):
            return ctx.enter_context(nc.semaphore(name))

        ps = ctx.enter_context(nc.psum_tensor("ps", [P, 8, BW], F32))

        ARENA = 27000
        arena = sb("arena", [P, ARENA], F32)
        place = {"A": 0, "B": 0}

        def carve(stage, words):
            at = place[stage]
            place[stage] = at + words
            assert place[stage] <= ARENA, (stage, place)
            return arena[:, at:at + words]

        xnT = sb("xnT", [P, KT, S], F32)
        idf = sb("idf", [P, P], F32)
        idb = sb("idb", [P, P], BF16)
        tri_sb = sb("tri_sb", [P, P], BF16)
        lr = sb("lr", [P, BW], F32)
        vall = sb("vall", [P, NH * QT * VW], F32)
        v4 = vall[:].rearrange("p (h t w) -> p h t w", h=NH, t=QT)
        kstack = sb("kstack", [P, RING, KC], BF16)
        qstack = sb("qstack", [P, RING, S], BF16)
        xs = carve("A", 8192)
        x_sb = xs.rearrange("p (t d) -> p t d", d=D)[:, 0:8, :]
        prod = xs[:, 0:4096].rearrange("p (s k c) -> p s k c", s=2, k=4)
        rot = xs[:, 4096:8192].rearrange("p (s k c) -> p s k c", s=4, k=2)
        w3 = carve("A", 3 * KT * D).rearrange("p (w k n) -> p w k n", w=3, k=KT)
        cs = carve("A", 2 * S).rearrange("p (k c) -> p k c", k=2)
        parts = carve("A", 4 * NPART * BW).bitcast(BF16).rearrange("p (s k a c) -> p s k a c", s=4, k=2, a=NPART)
        wlr_sb = carve("A", KT * 24).rearrange("p (k n) -> p k n", k=KT)
        ksum = carve("A", 2 * NC_).rearrange("p (k c) -> p k c", k=2)
        kmean = carve("A", 2 * NC_).rearrange("p (k c) -> p k c", k=2)
        kmp = carve("A", NPART * NC_).bitcast(BF16).rearrange("p (k a c) -> p k a c", k=2, a=NPART)
        stats = carve("A", 4 * 6).rearrange("p (t k) -> p t k", t=4)
        mv = carve("A", 4 * 2).rearrange("p (t k) -> p t k", t=4)
        rstd = carve("A", 4)
        LP = NE + 7
        lg = carve("A", QT * LP).rearrange("p (t e) -> p t e", t=QT)
        lghit = carve("A", QT * LP).rearrange("p (t e) -> p t e", t=QT)
        lmax8 = carve("A", QT * 8).rearrange("p (t e) -> p t e", t=QT)
        lexp = carve("A", QT * NE).rearrange("p (t e) -> p t e", t=QT)
        lsum = carve("A", QT)
        ew = carve("A", QT * NE).rearrange("p (t e) -> p t e", t=QT)
        ewT = carve("A", P)
        br_sb = carve("A", NE)
        prob = carve("B", 8 * BW).rearrange("p (s c) -> p s c", s=8)
        vst = carve("B", 2 * QT * VW).rearrange("p (s t w) -> p s t w", s=2, t=QT)
        stage = carve("B", NB * BW).rearrange("p (b c) -> p b c", b=NB)
        merged = carve("B", 2 * BW).rearrange("p (s c) -> p s c", s=2)
        GW = NC_ + TOPK
        gate = carve("B", QT * GW).rearrange("p (t c) -> p t c", t=QT)
        ghit = carve("B", QT * GW).rearrange("p (t c) -> p t c", t=QT)
        top8 = carve("B", QT * 8).rearrange("p (t e) -> p t e", t=QT)
        maskq = carve("B", QT * NC_ // 2).bitcast(BF16).rearrange("p (t c) -> p t c", t=QT)
        mxp = carve("B", 2 * QT * 4).rearrange("p (s t k) -> p s t k", s=2, t=QT)
        mx = carve("B", QT)
        nmax = carve("B", RING * P // 2).bitcast(BF16).rearrange("p (s c) -> p s c", s=RING)
        cbias_sb = carve("B", QT * NC_).rearrange("p (t c) -> p t c", t=QT)
        sel_sb = carve("B", VW)
        wo_sb = carve("B", KT * D).rearrange("p (k n) -> p k n", k=KT)
        wa_sb = carve("B", KT * D).rearrange("p (k n) -> p k n", k=KT)
        wb_sb = carve("B", KT * D).rearrange("p (k n) -> p k n", k=KT)
        wg2_sb = carve("B", D)
        hmean_sb = carve("B", P)
        onorm_sb = carve("B", 1)
        ewb = carve("B", 2 * KT * BW).rearrange("p (s k c) -> p s k c", s=2, k=KT)
        u_sb = vall[:, 0:4096].rearrange("p (s k c) -> p s k c", s=2, k=KT)
        l_sb = vall[:, 4096:8192].rearrange("p (s k c) -> p s k c", s=2, k=KT)
        qroom = qstack[:].rearrange("p s c -> p (s c)").bitcast(F32)
        kroom = kstack[:].rearrange("p s c -> p (s c)").bitcast(F32)
        sig = qroom[:, 0:2048].rearrange("p (k c) -> p k c", k=KT)
        hm = qroom[:, 2048:4096].rearrange("p (k c) -> p k c", k=KT)
        usq = kroom[:, 0:2048].rearrange("p (k c) -> p k c", k=KT)
        den = kroom[:, 2048:4096].rearrange("p (k c) -> p k c", k=KT)
        z = prob[:, 0:4, :]
        xres = prob[:, 4:8, :]
        osb = stage

        ld_x = [sem(f"ld_x{i}") for i in range(4)]
        ld_id = sem("ld_id")
        ld_w = sem("ld_w")
        ld_v = sem("ld_v")
        ld_b = sem("ld_b")
        ld_k = sem("ld_k")
        ln_step = sem("ln_step")
        ln_sqrt = sem("ln_sqrt")
        ln_ready = sem("ln_ready")
        tp_done = sem("tp_done")
        tp_read = sem("tp_read")
        proj_done = sem("proj_done")
        proj_read = sem("proj_read")
        rot_done = sem("rot_done")
        hi_done = sem("hi_done")
        res_done = sem("res_done")
        mid_done = sem("mid_done")
        lo_done = sem("lo_done")
        ks_done = sem("ks_done")
        km_step = sem("km_step")
        st_part = [sem(f"st_part{i}") for i in range(4)]
        st_km = sem("st_km")
        v_done = sem("v_done")
        v_read = sem("v_read")
        ones_set = sem("ones_set")
        lr_done = sem("lr_done")
        lr_read = sem("lr_read")
        lgT_done = sem("lgT_done")
        rt_step = sem("rt_step")
        rt_exp = sem("rt_exp")
        ewT_done = sem("ewT_done")
        ewT_read = sem("ewT_read")
        st_ew = sem("st_ew")
        ps_clear = sem("ps_clear")
        b_init = sem("b_init")
        ld_stack = [sem(f"ld_stack{i}") for i in range(RING)]
        ld_max = [sem(f"ld_max{i}") for i in range(RING)]
        s1_done = sem("s1_done")
        s1_read = sem("s1_read")
        s2_done = sem("s2_done")
        exp_done = sem("exp_done")
        tri_begun = sem("tri_begun")
        tri_done = sem("tri_done")
        pv_done = sem("pv_done")
        pv_read = sem("pv_read")
        v_staged = sem("v_staged")
        gates_done = sem("gates_done")
        misc_read = sem("misc_read")
        tk_step = sem("tk_step")
        mask_ready = sem("mask_ready")
        maskT_done = sem("maskT_done")
        mx_ready = sem("mx_ready")
        maxT_done = sem("maxT_done")
        merge_done = sem("merge_done")
        st_u = [sem(f"st_u{i}") for i in range(2)]
        ld_u = [sem(f"ld_u{i}") for i in range(2)]
        ld_ew = [sem(f"ld_ew{i}") for i in range(2)]
        ld_xr = sem("ld_xr")
        g_done = sem("g_done")
        sig_done = sem("sig_done")
        h_done = sem("h_done")
        hm_done = sem("hm_done")
        sq_done = sem("sq_done")
        l2_done = sem("l2_done")
        ms_done = sem("ms_done")
        sqrt_done = sem("sqrt_done")
        c_step = sem("c_step")
        den_read = sem("den_read")
        z_done = sem("z_done")
        o_done = sem("o_done")
        o_read = sem("o_read")
        st_o = sem("st_o")

        UNITS = [(g, n, w) for g in range(2) for n in range(NB) for w in range(2)]
        NU = len(UNITS)

        def pbank(u, half):
            return ps[:, 2 + (2 * u + half) % 4, :]

        S1 = [ps[:, b, :] for b in range(3)]
        S2 = [ps[:, 3 + b, :] for b in range(2)]
        PV = [ps[:, 5 + b, :] for b in range(2)]
        MISC = ps[:, 7, :]
        MISCB = MISC.bitcast(BF16)

        block = ctx.enter_context(nc.Block())

        @block.sync
        def _(sp):
            def load_x(b):
                sp.dma_start(x_sb[:, 4 * (b % 2):4 * (b % 2) + 4, :], xr[:, 4 * b:4 * b + 4, :]).then_inc(ld_x[b], 16)

            load_x(0)
            sp.dma_start(idf[:], identf).then_inc(ld_id, 16)
            load_x(1)
            for w in range(2):
                sp.dma_start(w3[:, w], wqkv[w]).then_inc(ld_w, 16)
            sp.dma_start(cs, rope).then_inc(ld_w, 16)
            for b in (2, 3):
                sp.wait_ge(tp_done, 4 * (b - 1))
                load_x(b)
            sp.dma_start(w3[:, 2], wqkv[2]).then_inc(ld_v, 16)
            sp.dma_start(wlr_sb, wlr).then_inc(ld_v, 16)
            sp.dma_start(br_sb, br.partition_broadcast(P)).then_inc(ld_v, 16)
            for s in range(RING):
                sp.dma_start(kstack[96:128, s, 0:S], krows).then_inc(ld_k, 16)
            sp.dma_start(idb[:], identb).then_inc(ld_k, 16)
            sp.dma_start(tri_sb[:], tri).then_inc(ld_k, 16)
            for u, (g, n, w) in enumerate(UNITS):
                sp.wait_ge(lo_done, u + 1)
                dst = (q_parts, k_parts)[w]
                for half in range(2):
                    for a in range(NPART):
                        sp.dma_start(
                            dst[16 * g:16 * g + 16, a, HH * half:HH * half + HH, n * BW:(n + 1) * BW],
                            parts[:, u % 4, half, a, :]).then_inc(st_part[u % 4], 16)
                if w == 1 and n == NB - 1:
                    sp.wait_ge(km_step, 6 * (g + 1))
                    for half in range(2):
                        for a in range(NPART):
                            sp.dma_start(
                                k_parts[16 * g:16 * g + 16, a, HH * half:HH * half + HH, S:KC],
                                kmp[:, half, a, :]).then_inc(st_km, 16)
            for s in range(4):
                sp.wait_ge(st_part[s], 96 * NU // 4)
            sp.wait_ge(st_km, 192)

            def load_stack(h, s):
                q, k = q_parts[bass.ds(h, 1)], k_parts[bass.ds(h, 1)]
                for dst, src in (
                        (kstack[0:48, s, :], k[:, 0].broadcast_to((3, HD, KC))),
                        (kstack[48:80, s, :], k[:, 1].broadcast_to((2, HD, KC))),
                        (kstack[80:96, s, :], k[:, 2]),
                        (qstack[0:48, s, :], q[:, 0:3]),
                        (qstack[48:80, s, :], q[:, 0:2]),
                        (qstack[80:96, s, :], q[:, 0])):
                    sp.dma_start(dst, src).then_inc(ld_stack[s], 16)

            load_stack(0, 0)

            def step(h, hs, hq, hi):
                ahead = h + 3
                if valid(ahead):
                    wait(sp, s2_done, NP_ * h)
                    load_stack(ahead, (hs + 3) % RING)
                if valid(h - 1):
                    sp.wait_ge(misc_read, misc_base(h, hi) + misc_slot("merge", hi) + 1)
                    sp.dma_start(u_dram[bass.ds(h - 1, 1)], merged[:, (hs - 1) % 2, :]).then_inc(st_u[(hs - 1) % 2], 16)
                if valid(h + 1):
                    sp.wait_ge(misc_read, misc_base(h, hi) + misc_slot("max", hi) + 1)
                    s = (hs + 1) % RING
                    sp.dma_start(qstack[127:128, s, :], nmax[0:QT, s, :]).then_inc(ld_max[s], 16)

            sp.wait_ge(ewT_read, 1)
            sp.dma_start(ew_dram.rearrange("e (t c) -> t e c", t=QT), ewT).then_inc(st_ew, 16)
            sp.wait_ge(st_ew, 16)
            sp.wait_ge(v_read, QT)
            sp.wait_ge(lr_read, 1)
            for dst, src in ((cbias_sb, cbias), (sel_sb, sel), (wo_sb, wo), (wa_sb, wa), (wb_sb, wb), (hmean_sb, hmean)):
                sp.dma_start(dst, src).then_inc(ld_b, 16)
            for b in range(NB):
                sp.dma_start(wg2_sb[32 * b:32 * b + 16, :], wg2).then_inc(ld_b, 16)
            for g in range(8):
                sp.dma_start(onorm_sb[16 * g:16 * g + 16, :], onorm).then_inc(ld_b, 16)

            def load_ew(n):
                for m in range(KT):
                    sp.dma_start(ewb[:, n % 2, m, :], ew_dram[2 * m:2 * m + 2, n * BW:(n + 1) * BW].unsqueeze(1)
                                 .broadcast_to((2, RANK, BW))).then_inc(ld_ew[n % 2], 16)

            load_ew(0)
            load_ew(1)
            all_steps(sp, step)

            for s in range(2):
                sp.wait_ge(st_u[s], 16 * NH // 2)
            for n in range(NB):
                if n >= 2:
                    sp.wait_ge(z_done, KT * (n - 1))
                s = n % 2
                for j in range(KT):
                    src = u_dram[8 * j:8 * j + 8]
                    sp.dma_start(u_sb[:, s, j, :], src[:, 32 * n:32 * n + HD, :]).then_inc(ld_u[s], 16)
                    sp.dma_start(l_sb[:, s, j, :], src[:, 32 * n + HD:32 * n + HD + 1, :]
                                 .broadcast_to((8, HD, BW))).then_inc(ld_u[s], 16)
                if n >= 1:
                    sp.wait_ge(o_read, 4 * n)
                sp.dma_start(xres, xr[:, 4 * n:4 * n + 4, :]).then_inc(ld_xr, 16)
                if n >= 1:
                    for t in range(4 * n - 4, 4 * n):
                        sp.dma_start(outr[:, t, :], osb[:, t % 4, :]).then_inc(st_o, 16)
                if n >= 2:
                    sp.wait_ge(hm_done, KT * (n - 1))
                    load_ew(n)
            sp.wait_ge(o_read, QT)
            for t in range(QT - 4, QT):
                sp.dma_start(outr[:, t, :], osb[:, t % 4, :]).then_inc(st_o, 16)
            sp.wait_ge(st_o, 16 * QT)

        @block.tensor
        def _(pe):
            pe.wait_ge(ld_id, 16)
            pe.wait_ge(ps_clear, 1)
            for n in range(4 * NB):
                b, k = n // 4, n % 4
                pe.wait_ge(ln_ready, 4 * (b + 1))
                wait(pe, tp_read, n - 1)
                for t in range(4):
                    mm = pe.transpose(ps[:, n % 2, t * P:(t + 1) * P], x_sb[:, 4 * (b % 2) + t, k * P:(k + 1) * P], idf[:])
                mm.then_inc(tp_done, 1)
            pe.wait_ge(ld_w, 16 * 3)
            for u, (g, n, w) in enumerate(UNITS):
                pe.wait_ge(tp_read, min(4 * NB, 4 * (n + 1)))
                wait(pe, proj_read, u - 1)
                for half in range(2):
                    for k in range(KT):
                        m = 2 * g + half
                        mm = pe.matmul(pbank(u, half), w3[:, w, k, m * P:(m + 1) * P], xnT[:, k, n * BW:(n + 1) * BW],
                                       start=(k == 0), stop=(k == KT - 1))
                mm.then_inc(proj_done, 1)
            pe.wait_ge(ld_v, 16 * 3)
            for k in range(KT):
                for n in range(NB):
                    mm = pe.matmul(ps[32 * n:32 * n + 24, 6, :], wlr_sb[:, k, :], xnT[:, k, n * BW:(n + 1) * BW],
                                   start=(k == 0), stop=(k == KT - 1), tile_position=(0, 32 * n))
            mm.then_inc(lr_done, 1)
            for t in range(QT):
                if t < 4:
                    wait(pe, proj_read, NU)
                wait(pe, v_read, t - 3)
                for k in range(KT):
                    mm = pe.matmul(ps[:, 2 + t % 4, :], xnT[:, k, t * P:(t + 1) * P], w3[:, 2, k, :],
                                   start=(k == 0), stop=(k == KT - 1))
                mm.then_inc(v_done, 1)
                if t == 1:
                    pe.wait_ge(lr_read, 1)
                    for s in range(4):
                        mm = pe.transpose(MISC[:, s * P:(s + 1) * P], lr[:, s * P:(s + 1) * P], idf[:])
                    mm.then_inc(lgT_done, 1)
            pe.wait_ge(rt_step, 7)
            pe.transpose(ps[:, 6, 0:P], ew.rearrange("p t e -> p (t e)"), idf[:]).then_inc(ewT_done, 1)

            pe.wait_ge(ld_k, 16 * (RING + 2))
            pe.wait_ge(b_init, 1)
            pe.wait_ge(v_read, QT)
            pe.wait_ge(ewT_read, 1)
            pe.wait_ge(ld_b, 16 * 18)

            def piece(h, hs, n):
                i, p = PIECES[n]
                s, bank = hs % RING, S1[BANK1[n]]
                wait(pe, s1_read, NP_ * h + (n - bank1_before(n) + 1))
                last = p == i // 4
                w = (i % 4 + 1) * P if last else BW
                mm = pe.matmul(bank[:, 0:w], qstack[0:127, s, i * P:(i + 1) * P], kstack[0:127, s, p * BW:p * BW + w],
                               start=True, stop=not last)
                if last:
                    mm = pe.matmul(bank[:, w - P:w], idb[:], tri_sb[:], start=False, stop=True)
                mm.then_inc(s1_done, 1)

            def tile(h, hs, n):
                b, j = TILES[n]
                s, r = hs % RING, max(0, j - 4 * b)
                wait(pe, exp_done, NP_ * h + (n - 1))
                w = BW - r * P
                pe.matmul(S2[n % 2][:, 0:w], kstack[:, s, j * P:(j + 1) * P], qstack[:, s, b * BW + r * P:(b + 1) * BW],
                          start=True, stop=True).then_inc(s2_done, 1)

            def values(h, hs, g):
                b = TILES[4 * g][0]
                if g == 0:
                    pe.wait_ge(v_staged, h + 1)
                pe.wait_ge(exp_done, NP_ * h + 4 * (g + 1))
                if g in LAST_GROUP:
                    pe.wait_ge(tri_done, QT * h + 4 * (b + 1))
                if TILES[4 * g][1] == 0:
                    wait(pe, pv_read, NB * h + (b - 1))
                for t in range(4):
                    n = 4 * g + t
                    j = TILES[n][1]
                    r = max(0, j - 4 * b)
                    mm = pe.matmul(PV[b % 2][32 * t:32 * t + VW, r * P:BW], vst[:, hs % 2, j, :],
                                   prob[:, n % 8, 0:BW - r * P], start=(j < 4), stop=(g in LAST_GROUP),
                                   tile_position=(0, 32 * t))
                mm.then_inc(pv_done, 1)

            def step(h, hs, hq, hi):
                base = misc_base(h, hi)

                def turn(off):
                    return hq + (hs + off) // RING + 1

                for g in range(NG):
                    ahead = (g + LEAD) // NG + 1
                    for t in range(4):
                        if valid(h + ahead):
                            n = 4 * ((g + LEAD) % NG) + t
                            if n == 0:
                                pe.wait_ge(misc_read, base + misc_slot("mask0", hi) + 1)
                            if PIECES[n] == (QT // 2, 0):
                                pe.wait_ge(misc_read, misc_base(h - 1, None if hi is None or hi >= 2 else hi - 1)
                                           + misc_slot("mask1", None if hi is None or hi >= 2 else hi - 1) + 1)
                            piece(h + ahead, hs + ahead, n)
                        if valid(h):
                            n = 4 * g + t
                            if n == 0:
                                pe.wait_ge(ld_max[hs % RING], 16 * turn(0))
                            tile(h, hs, n)
                        if g == 8 and t == 1 and valid(h + 1):
                            pe.wait_ge(mx_ready, h + 2)
                            wait(pe, misc_read, base + misc_slot("max", hi))
                            pe.transpose(MISC[0:QT, 0:P], mx, idf[:]).then_inc(maxT_done, 1)
                    if g > 0 and valid(h):
                        values(h, hs, g - 1)
                    if g == 0 and valid(h - 1):
                        values(h - 1, hs - 1, NG - 1)
                    if g == 0 and valid(h + 2):
                        s = (hs + 2) % RING
                        pe.wait_ge(ld_stack[s], 96 * turn(2))
                        wait(pe, misc_read, base + misc_slot("gates", hi))
                        for i in range(QT):
                            mm = pe.matmul(MISC[:, i * NC_:(i + 1) * NC_], qstack[0:96, s, i * P:(i + 1) * P],
                                           kstack[0:96, s, S:KC], start=True, stop=True)
                        mm.then_inc(gates_done, 1)
                    if g == 1 and valid(h - 1):
                        pe.wait_ge(pv_read, NB * h)
                        wait(pe, misc_read, base + misc_slot("merge", hi))
                        for b in range(NB):
                            mm = pe.matmul(MISC[32 * b:32 * b + VW, :], sel_sb, stage[:, b, :],
                                           start=True, stop=True, tile_position=(0, 32 * b))
                        mm.then_inc(merge_done, 1)
                    if g in (5, 6) and valid(h + 2):
                        half = g - 5
                        if half == 0:
                            pe.wait_ge(mask_ready, h + 3)
                        wait(pe, misc_read, base + misc_slot(f"mask{half}", hi))
                        for i in range(QT // 2):
                            mm = pe.transpose(MISCB[96:128, i * P:(i + 1) * P], maskq[:, half * QT // 2 + i, :],
                                              idb[:], tile_position=(0, 96))
                        mm.then_inc(maskT_done, 1)

            all_steps(pe, step)

            pe.wait_ge(exp_done, NP_ * NH)
            pe.wait_ge(pv_read, NB * NH)
            pe.wait_ge(misc_read, misc_base(32, 32) + 1)
            for n in range(NB):
                for j in range(KT):
                    q = 4 * n + j
                    wait(pe, sig_done, q - 1)
                    pe.matmul(ps[:, q % 2, :], wg2_sb[32 * n:32 * n + 16, j * P:(j + 1) * P], lr[32 * n:32 * n + 16, :],
                              start=True, stop=True, tile_position=(32 * n, 0)).then_inc(g_done, 1)
                for m in range(KT):
                    q = 4 * n + m
                    wait(pe, hm_done, q - 1)
                    for k in range(KT):
                        mm = pe.matmul(ps[:, 2 + q % 2, :], wa_sb[:, k, m * P:(m + 1) * P], xnT[:, k, n * BW:(n + 1) * BW],
                                       start=(k == 0), stop=(k == KT - 1))
                    mm.then_inc(h_done, 1)
                for j in range(KT):
                    q = 4 * n + j
                    pe.wait_ge(sq_done, q + 1)
                    wait(pe, den_read, q - 1)
                    pe.matmul(ps[:, 4 + q % 2, :], hmean_sb, usq[:, j, :], start=True, stop=True).then_inc(ms_done, 1)
                pe.wait_ge(z_done, KT * (n + 1))
                pe.wait_ge(hm_done, KT * (n + 1))
                for t in range(4):
                    q = 4 * n + t
                    wait(pe, o_read, q - 1)
                    for k in range(KT):
                        pe.matmul(ps[:, 6 + q % 2, :], hm[:, k, t * P:(t + 1) * P], wb_sb[:, k, :], start=(k == 0), stop=False)
                    for k in range(KT):
                        mm = pe.matmul(ps[:, 6 + q % 2, :], z[:, k, t * P:(t + 1) * P], wo_sb[:, k, :],
                                       start=False, stop=(k == KT - 1))
                    mm.then_inc(o_done, 1)

        @block.scalar
        def _(act):
            for n in range(4 * NB):
                if n % 4 == 0:
                    act.wait_ge(ln_step, n + 3)
                    nc.scalar.activation(rstd, rstd, ACT.Sqrt).then_inc(ln_sqrt, 1)
                act.wait_ge(tp_done, n + 1)
                nc.scalar.copy(xnT[:, n % 4, (n // 4) * BW:(n // 4 + 1) * BW], ps[:, n % 2, :]).then_inc(tp_read, 1)
            for u in range(NU + 1):
                if u < NU:
                    act.wait_ge(rot_done, u + 1)
                    if u >= 4:
                        act.wait_ge(st_part[u % 4], 96 * (u // 4))
                    nc.scalar.copy(parts[:, u % 4, :, 0, :], rot[:, u % 4]).then_inc(hi_done, 1)
                if u >= 1:
                    act.wait_ge(res_done, u)
                    nc.scalar.copy(parts[:, (u - 1) % 4, :, 1, :], rot[:, (u - 1) % 4]).then_inc(mid_done, 1)
            act.wait_ge(lr_done, 1)
            nc.scalar.copy(lr[:], ps[:, 6, :]).then_inc(lr_read, 1)
            act.wait_ge(ones_set, 1)
            for t in range(QT):
                act.wait_ge(v_done, t + 1)
                nc.scalar.copy(v4[:, :, t, 0:HD], ps[:, 2 + t % 4, :].rearrange("p (h d) -> p h d", h=NH)).then_inc(v_read, 1)
                if t == 4:
                    act.wait_ge(rt_step, 3)
                    nc.scalar.activation(lexp, lexp, ACT.Exp).then_inc(rt_exp, 1)
            act.wait_ge(ewT_done, 1)
            nc.scalar.copy(ewT, ps[:, 6, 0:P]).then_inc(ewT_read, 1)

            act.wait_ge(b_init, 1)

            def evac(h, b, g):
                act.wait_ge(pv_done, NG * h + g + 1)
                if b == 0:
                    wait(act, merge_done, h)
                    for r in range(4):
                        cp = nc.scalar.copy(stage[0:32 * (r + 1), 0, r * P:(r + 1) * P],
                                            PV[0][0:32 * (r + 1), r * P:(r + 1) * P])
                else:
                    cp = nc.scalar.copy(stage[:, b, :], PV[b % 2])
                cp.then_inc(pv_read, 1)

            def step(h, hs, hq, hi):
                base = misc_base(h, hi)
                for g in range(NG):
                    for t in range(4):
                        if t == 2 and g in (6, 7) and valid(h + 2):
                            half = g - 6
                            act.wait_ge(maskT_done, 2 * (h + 2) + half + 1)
                            nc.scalar.copy(qstack[96:128, (hs + 2) % RING, half * 1024:(half + 1) * 1024],
                                           MISCB[96:128, :]).then_inc(misc_read, 1)
                        if not valid(h):
                            continue
                        n = 4 * g + t
                        b, j = TILES[n]
                        w = BW - max(0, j - 4 * b) * P
                        if t == 0:
                            wait(act, pv_done, NG * h + (g - 1))
                        act.wait_ge(s2_done, NP_ * h + n + 1)
                        nc.scalar.activation(prob[:, n % 8, 0:w], S2[n % 2][:, 0:w], ACT.Exp,
                                             scale=float(HD) ** -0.5).then_inc(exp_done, 1)
                    if g == 0 and valid(h - 1):
                        evac(h - 1, NB - 1, NG - 1)
                    if g - 1 in LAST_GROUP and valid(h):
                        evac(h, LAST_GROUP[g - 1], g - 1)
                    if g == 2 and valid(h - 1):
                        act.wait_ge(merge_done, h)
                        if hi is None or hi >= 3:
                            act.wait_ge(st_u[(hs - 1) % 2], (hq * 2 + (hs - 1) // 2) * 16)
                        nc.scalar.copy(merged[:, (hs - 1) % 2, :], MISC).then_inc(misc_read, 1)

            all_steps(act, step)

            for n in range(NB):
                act.wait_ge(ld_u[n % 2], 128 * (n // 2 + 1))
                if n >= 1:
                    act.wait_ge(z_done, KT * n)
                for j in range(KT):
                    nc.scalar.activation(usq[:, j, :], u_sb[:, n % 2, j, :], ACT.Square).then_inc(sq_done, 1)
                for j in range(KT):
                    nc.scalar.activation(den[:, j, :], l_sb[:, n % 2, j, :], ACT.Square,
                                         scale=RMS_EPS ** 0.5).then_inc(l2_done, 1)
                for j in range(KT):
                    q = 4 * n + j
                    act.wait_ge(g_done, q + 1)
                    nc.scalar.activation(sig[:, j, :], ps[:, q % 2, :], ACT.Sigmoid).then_inc(sig_done, 1)
                for j in range(KT):
                    q = 4 * n + j
                    act.wait_ge(den_read, q + 1)
                    nc.scalar.activation(den[:, j, :], den[:, j, :], ACT.Sqrt).then_inc(sqrt_done, 1)

        @block.vector
        def _(dve):
            nc.vector.memset(ps[:], 0.0).then_inc(ps_clear, 1)
            links = 0
            for b in range(NB):
                dve.wait_ge(ld_x[b], 16)
                sl = 4 * (b % 2)
                for t in range(4):
                    cp = nc.vector.bn_stats(stats[:, t, :], x_sb[:, sl + t, :])
                cp.then_inc(ln_step, 1)
                links += 1
                dve.wait_ge(ln_step, links)
                for t in range(4):
                    cp = nc.vector.bn_aggr(mv[:, t, :], stats[:, t, :])
                cp.then_inc(ln_step, 1)
                links += 1
                dve.wait_ge(ln_step, links)
                nc.vector.tensor_scalar(rstd, mv[:, :, 1], LN_EPS, None, ALU.add).then_inc(ln_step, 1)
                links += 1
                dve.wait_ge(ln_sqrt, b + 1)
                nc.vector.reciprocal(rstd, rstd).then_inc(ln_step, 1)
                links += 1
                dve.wait_ge(ln_step, links)
                for t in range(4):
                    nc.vector.tensor_scalar(x_sb[:, sl + t, :], x_sb[:, sl + t, :], mv[:, t, 0:1], rstd[:, t:t + 1],
                                            ALU.subtract, ALU.mult).then_inc(ln_ready, 1)
            dve.wait_ge(tp_done, 4 * NB)

            def mean_keys(g):
                base = 6 * g
                if g:
                    dve.wait_ge(st_km, 96)
                dve.wait_ge(res_done, 8 * g + 8)
                nc.vector.tensor_scalar(kmean, ksum, 1.0 / CH, None, ALU.mult).then_inc(km_step, 1)
                dve.wait_ge(km_step, base + 1)
                nc.vector.tensor_copy(kmp[:, :, 0, :], kmean).then_inc(km_step, 1)
                dve.wait_ge(km_step, base + 2)
                nc.vector.tensor_tensor(kmean, kmean, kmp[:, :, 0, :], ALU.subtract).then_inc(km_step, 1)
                dve.wait_ge(km_step, base + 3)
                nc.vector.tensor_copy(kmp[:, :, 1, :], kmean).then_inc(km_step, 1)
                dve.wait_ge(km_step, base + 4)
                nc.vector.tensor_tensor(kmean, kmean, kmp[:, :, 1, :], ALU.subtract).then_inc(km_step, 1)
                dve.wait_ge(km_step, base + 5)
                nc.vector.tensor_copy(kmp[:, :, 2, :], kmean).then_inc(km_step, 1)

            dve.wait_ge(ld_w, 16 * 3)
            for u in range(NU + 2):
                if u < NU:
                    n = UNITS[u][1]
                    dve.wait_ge(proj_done, u + 1)
                    wait(dve, rot_done, u - 1)
                    lo, hi = pbank(u, 0), pbank(u, 1)
                    cos, sin = cs[:, 0, n * BW:(n + 1) * BW], cs[:, 1, n * BW:(n + 1) * BW]
                    nc.vector.tensor_tensor(prod[:, u % 2, 0], lo, cos, ALU.mult)
                    nc.vector.tensor_tensor(prod[:, u % 2, 1], hi, sin, ALU.mult)
                    nc.vector.tensor_tensor(prod[:, u % 2, 2], lo, sin, ALU.mult)
                    nc.vector.tensor_tensor(prod[:, u % 2, 3], hi, cos, ALU.mult).then_inc(proj_read, 1)
                if 1 <= u <= NU:
                    v = u - 1
                    g, n, w = UNITS[v]
                    dve.wait_ge(hi_done, v + 1)
                    if w == 1:
                        if n == 0 and g:
                            dve.wait_ge(km_step, 6 * g)
                        nc.vector.tensor_reduce(ksum[:, :, 8 * n:8 * n + 8],
                                                rot[:, v % 4].rearrange("p a (c k) -> p a c k", k=CH), AX.X,
                                                ALU.add).then_inc(ks_done, 1)
                        dve.wait_ge(ks_done, NB * g + n + 1)
                    nc.vector.tensor_tensor(rot[:, v % 4], rot[:, v % 4], parts[:, v % 4, :, 0, :],
                                            ALU.subtract).then_inc(res_done, 1)
                if u >= 2:
                    v = u - 2
                    g, n, w = UNITS[v]
                    dve.wait_ge(mid_done, v + 1)
                    nc.vector.tensor_tensor(parts[:, v % 4, :, 2, :], rot[:, v % 4], parts[:, v % 4, :, 1, :],
                                            ALU.subtract).then_inc(lo_done, 1)
                    if w == 1 and n == NB - 1:
                        mean_keys(g)
            nc.vector.memset(lg[:, :, NE:LP], SENT)
            nc.vector.memset(lmax8, SENT)
            dve.wait_ge(ld_v, 16 * 3)
            dve.wait_ge(lgT_done, 1)
            nc.vector.tensor_tensor(
                lg[:, :, 0:NE].rearrange("p (q s) e -> p q s e", q=4),
                MISC.rearrange("p (s q r) -> p q s r", s=4, q=4)[:, :, :, 16:16 + NE],
                br_sb.unsqueeze(1).unsqueeze(1).broadcast_to((P, 4, 4, NE)), ALU.add).then_inc(rt_step, 1)
            dve.wait_ge(rt_step, 1)
            nc.vector.tensor_reduce(lmax8[:, :, 0:1], lg[:, :, 0:NE], AX.X, ALU.max).then_inc(rt_step, 1)
            dve.wait_ge(rt_step, 2)
            for t in range(QT):
                nc.vector.match_replace(lghit[:, t, :], lmax8[:, t, :], lg[:, t, :], HIT)
            nc.vector.tensor_tensor(lexp, lg[:, :, 0:NE], lmax8[:, :, 0:1].broadcast_to((P, QT, NE)),
                                    ALU.subtract).then_inc(rt_step, 1)
            dve.wait_ge(rt_exp, 1)
            nc.vector.tensor_reduce(lsum, lexp, AX.X, ALU.add).then_inc(rt_step, 1)
            dve.wait_ge(rt_step, 4)
            nc.vector.tensor_scalar(lsum, lsum, float(RANK), None, ALU.mult).then_inc(rt_step, 1)
            dve.wait_ge(rt_step, 5)
            nc.vector.reciprocal(lsum, lsum).then_inc(rt_step, 1)
            dve.wait_ge(rt_step, 6)
            nc.vector.scalar_tensor_tensor(out=ew, in0=lghit[:, :, 0:NE], scalar=HIT,
                                           in1=lsum.unsqueeze(2).broadcast_to((P, QT, NE)),
                                           op0=ALU.is_equal, op1=ALU.mult).then_inc(rt_step, 1)

            dve.wait_ge(ewT_done, 1)
            dve.wait_ge(v_read, QT)
            dve.wait_ge(ewT_read, 1)
            for s in range(4):
                dve.wait_ge(st_part[s], 96 * NU // 4)
            nc.vector.memset(stage[:, 0, :], 0.0)
            nc.vector.memset(mxp, -SENT)
            nc.vector.memset(gate[:, :, NC_:GW], SENT).then_inc(b_init, 1)
            dve.wait_ge(b_init, 1)
            dve.wait_ge(ld_b, 16 * 18)

            def step(h, hs, hq, hi):
                base = misc_base(h, hi)
                for g in range(NG):
                    ahead = (g + LEAD) // NG + 1
                    for t in range(4):
                        if valid(h + ahead):
                            n = 4 * ((g + LEAD) % NG) + t
                            i, p = PIECES[n]
                            w = (i % 4 + 1) * P if p == i // 4 else BW
                            dve.wait_ge(s1_done, NP_ * (h + ahead) + n + 1)
                            nc.vector.tensor_reduce(mxp[:, (hs + ahead) % 2, i, p:p + 1], S1[BANK1[n]][:, 0:w], AX.X,
                                                    ALU.max).then_inc(s1_read, 1)
                    if g == NG - 1 - LEAD and valid(h + 1):
                        dve.wait_ge(s1_read, NP_ * (h + 2))
                        wait(dve, maxT_done, h + 1)
                        nc.vector.tensor_reduce(mx, mxp[:, (hs + 1) % 2], AX.X, ALU.max).then_inc(mx_ready, 1)
                    if g == 8 and valid(h + 1):
                        dve.wait_ge(maxT_done, h + 2)
                        nc.vector.tensor_scalar(nmax[0:QT, (hs + 1) % RING, :], MISC[0:QT, 0:P], -1.0, None,
                                                ALU.mult).then_inc(misc_read, 1)
                    if not valid(h + 2):
                        continue
                    links = 3 * (h + 2)
                    if g == 0:
                        dve.wait_ge(gates_done, h + 3)
                        nc.vector.tensor_tensor(gate[:, :, 0:NC_], MISC.rearrange("p (t c) -> p t c", t=QT), cbias_sb,
                                                ALU.add).then_inc(misc_read, 1)
                        dve.wait_ge(misc_read, base + misc_slot("gates", hi) + 1)
                    if g in (1, 2):
                        for i in range((g - 1) * 8, g * 8):
                            cp = nc.vector.max(top8[:, i, :], gate[:, i, 0:NC_])
                        if g == 2:
                            cp.then_inc(tk_step, 1)
                            dve.wait_ge(tk_step, links + 1)
                            nc.vector.memset(top8[:, :, TOPK:8], SENT).then_inc(tk_step, 1)
                            dve.wait_ge(tk_step, links + 2)
                    if g in (3, 4):
                        for i in range((g - 3) * 8, (g - 2) * 8):
                            cp = nc.vector.match_replace(ghit[:, i, :], top8[:, i, :], gate[:, i, :], HIT)
                        if g == 4:
                            cp.then_inc(tk_step, 1)
                            dve.wait_ge(tk_step, links + 3)
                            wait(dve, maskT_done, 2 * (h + 2))
                            nc.vector.tensor_scalar(maskq, ghit[:, :, 0:NC_], HIT, MASK, ALU.not_equal,
                                                    ALU.mult).then_inc(mask_ready, 1)

            all_steps(dve, step)

            links = 0
            for n in range(NB):
                dve.wait_ge(ld_ew[n % 2], 64 * (n // 2 + 1))
                if n >= 1:
                    dve.wait_ge(o_done, 4 * n)
                for m in range(KT):
                    q = 4 * n + m
                    dve.wait_ge(h_done, q + 1)
                    nc.vector.tensor_tensor(hm[:, m, :], ps[:, 2 + q % 2, :], ewb[:, n % 2, m, :], ALU.mult).then_inc(hm_done, 1)
                for j in range(KT):
                    q = 4 * n + j
                    dve.wait_ge(ms_done, q + 1)
                    dve.wait_ge(l2_done, q + 1)
                    nc.vector.tensor_tensor(den[:, j, :], ps[:, 4 + q % 2, :], den[:, j, :], ALU.add).then_inc(den_read, 1)
                for j in range(KT):
                    q = 4 * n + j
                    dve.wait_ge(sqrt_done, q + 1)
                    nc.vector.reciprocal(den[:, j, :], den[:, j, :]).then_inc(c_step, 1)
                    dve.wait_ge(c_step, 2 * q + 1)
                    nc.vector.tensor_tensor(den[:, j, :], den[:, j, :], u_sb[:, n % 2, j, :], ALU.mult).then_inc(c_step, 1)
                    dve.wait_ge(c_step, 2 * q + 2)
                    dve.wait_ge(sig_done, q + 1)
                    nc.vector.scalar_tensor_tensor(out=z[:, j, :], in0=den[:, j, :], scalar=onorm_sb, in1=sig[:, j, :],
                                                   op0=ALU.mult, op1=ALU.mult).then_inc(z_done, 1)
                dve.wait_ge(ld_xr, 16 * (n + 1))
                if n >= 1:
                    dve.wait_ge(st_o, 64 * n)
                for t in range(4):
                    q = 4 * n + t
                    dve.wait_ge(o_done, q + 1)
                    nc.vector.tensor_tensor(osb[:, t, :], ps[:, 6 + q % 2, :], xres[:, t, :], ALU.add).then_inc(o_read, 1)

        @block.gpsimd
        def _(pool):
            nc.gpsimd.memset(v4[:, :, :, HD:VW], 1.0).then_inc(ones_set, 1)
            for u in range(NU):
                pool.wait_ge(proj_read, u + 1)
                wait(pool, lo_done, u - 3)
                nc.gpsimd.tensor_tensor(rot[:, u % 4, 0], prod[:, u % 2, 0], prod[:, u % 2, 1], ALU.subtract)
                nc.gpsimd.tensor_tensor(rot[:, u % 4, 1], prod[:, u % 2, 2], prod[:, u % 2, 3], ALU.add).then_inc(rot_done, 1)
            pool.wait_ge(b_init, 1)
            pool.wait_ge(v_read, QT)

            def step(h, hs, hq, hi):
                for g in range(NG):
                    if g == 4 and valid(h + 1):
                        wait(pool, pv_done, NG * h)
                        nc.gpsimd.tensor_copy(vst[:, (hs + 1) % 2].rearrange("p t w -> p (t w)"),
                                              vall[:].rearrange("p (h w) -> p h w", h=NH)[:, bass.ds(h + 1, 1), :]
                                              .rearrange("p h w -> p (h w)")).then_inc(v_staged, 1)
                    if not valid(h):
                        continue
                    for t in range(4):
                        n = 4 * g + t
                        b, j = TILES[n]
                        if j >= 4 * b:
                            pool.wait_ge(exp_done, NP_ * h + n + 1)
                            pool.sem_inc(tri_begun, 1)
                            pb = prob[:, n % 8, 0:P]
                            nc.gpsimd.affine_select(out=pb, in_=pb, compare_op=ALU.is_ge, fill=0.0, base=0,
                                                    pattern=[[1, P]], channel_multiplier=-1).then_inc(tri_done, 1)

            all_steps(pool, step)


def kernel(L0_attn_hidden_states, L0_attn_Wq, L0_attn_Wk, L0_attn_Wv, L0_attn_Wo, L0_attn_Wg1, L0_attn_Wg2,
           L0_attn_o_norm_weight, L0_ffn_A, L0_ffn_B, L0_ffn_Wr, L0_ffn_br):
    import ml_dtypes
    import concourse.bacc as bacc
    from concourse.bass_utils import run_bass_kernel_spmd

    def tiled(w):
        return np.ascontiguousarray(w.reshape(KT, P, -1).transpose(1, 0, 2))

    x = np.ascontiguousarray(L0_attn_hidden_states)
    halves = np.arange(D).reshape(2, 16, 2, HH).transpose(0, 2, 1, 3).reshape(-1)
    wqkv = np.stack([tiled(np.asarray(L0_attn_Wq).T[:, halves]), tiled(np.asarray(L0_attn_Wk).T[:, halves]),
                     tiled(np.asarray(L0_attn_Wv).T)])
    wlr = tiled(np.concatenate([np.asarray(L0_attn_Wg1).T, np.asarray(L0_ffn_Wr).T], axis=1))
    bf = ml_dtypes.bfloat16
    pos = np.arange(S, dtype=np.float32)
    inv = (np.float32(1.0) / np.float32(10000.0) ** (np.arange(0, HD, 2, dtype=np.float32) / np.float32(HD))).astype(np.float32)
    ang = pos[None, :] * inv[:, None]
    rope = np.tile(np.stack([np.cos(ang), np.sin(ang)], axis=1), (16, 1, 1)).astype(np.float32)
    krows = (np.arange(NC_)[:, None] == np.arange(S)[None, :] // CH).astype(bf)
    krows[NC_ - 1] = 1
    tok = (np.arange(QT)[None, :] * P + np.arange(P)[:, None]) // CH
    ids = np.arange(NC_)[None, None, :]
    cbias = np.where(ids > tok[:, :, None], NEG, np.where(ids == tok[:, :, None], -NEG, 0.0)).astype(np.float32)
    tri = np.where(np.arange(P)[None, :] > np.arange(P)[:, None], MASK, 0.0).astype(bf)
    sel = np.zeros((P, VW), np.float32)
    for r in range(4):
        sel[32 * r:32 * r + VW] = np.eye(VW)
    hmean = np.kron(np.eye(8), np.full((HD, HD), 1.0 / HD)).astype(np.float32)
    arrays = {
        "x": x, "wqkv": wqkv, "wlr": wlr, "wg2": np.ascontiguousarray(np.asarray(L0_attn_Wg2).T),
        "wo": tiled(np.asarray(L0_attn_Wo).T), "wa": tiled(np.asarray(L0_ffn_A).reshape(NE * RANK, D).T),
        "wb": tiled(np.asarray(L0_ffn_B).transpose(0, 2, 1).reshape(NE * RANK, D)),
        "onorm": np.asarray(L0_attn_o_norm_weight).reshape(HD, 1), "br": np.asarray(L0_ffn_br),
        "rope": rope, "krows": krows, "cbias": cbias, "identf": np.eye(P, dtype=np.float32),
        "identb": np.eye(P).astype(bf), "tri": tri, "sel": sel, "hmean": hmean,
    }
    nc = bacc.Bacc("TRN2", target_bir_lowering=False, num_devices=1)
    args = [nc.dram_tensor(n, a.shape, mybir.dt.from_np(a.dtype), kind="ExternalInput").ap() for n, a in arrays.items()]
    out = nc.dram_tensor("out", x.shape, F32, kind="ExternalOutput").ap()
    nc.disable_value_cache = True
    build(nc, *args, out)
    r = run_bass_kernel_spmd(nc, [arrays], core_ids=[0])
    return r.results[0]["out"]
```

```python
from contextlib import ExitStack

import numpy as np

import concourse.bass as bass
from concourse import mybir

P = 128
S = 2048
D = 512
NH = 32
HD = 16
HH = HD // 2
CH = 64
NC_ = S // CH
TOPK = 4
NE = 8
RANK = 64
NEG = -1e30
MASK = -float(2 ** 46)
KT = D // P
QT = S // P
BW = 512
NB = S // BW
VW = HD + 1
KC = S + NC_
SENT = 3.0e38
HIT = 2.0e38
RMS_EPS = 1e-6
LN_EPS = 1e-5
NPART = 3
RING = 4

F32 = mybir.dt.float32
BF16 = mybir.dt.bfloat16
ALU = mybir.AluOpType
ACT = mybir.ActivationFunctionType
AX = mybir.AxisListType

PIECES = [(i, p) for i in range(QT) for p in range(i // 4 + 1)]
TILES = [(b, j) for b in range(NB) for j in range(4 * b + 4)]
NP_ = len(PIECES)
NG = NP_ // 4
assert len(TILES) == NP_ and NP_ % 8 == 0
LAST_GROUP = {sum(1 for t in TILES if t[0] <= b) // 4 - 1: b for b in range(NB)}
BANK = [n % 3 for n in range(NP_)]
BANK[NP_ - 1] = 1
LEAD = 3
FIRST, LAST = -3, NH

TOP_AT = [(8 + i // 12, i % 12 // 3) for i in range(QT)]
CLEAR_AT = 0
MATCH_AT = [divmod(4 + i // 3, 4) for i in range(QT)]
MASKS_AT = (4, 5)
GATES_AT = 6
EVAC_AT = (1, 3, 6)
MAX_AT = (8, 0)
V_AT = [(-3, g) for g in range(4)] + [(-2, g) for g in (0, 2, 4, 5, 6, 8)] + [(-1, g) for g in range(6)]
assert len(V_AT) == QT


def bank_before(n):
    k = 1
    while BANK[(n - k) % NP_] != BANK[n]:
        k += 1
    return k


def misc_uses(hi):
    def there(h):
        return hi is None or 0 <= hi + h < NH
    return (["merge"] * there(-1) + ["mask0", "mask1"] * there(2) + ["gates"] * there(3) + ["max"] * there(1))


def misc_count(h, hi, what):
    if hi is None or 1 <= hi <= NH - 3:
        before = sum(len(misc_uses(g)) for g in range(FIRST, 1)) + 5 * (h - 1)
    else:
        before = sum(len(misc_uses(g)) for g in range(FIRST, hi))
    return before + misc_uses(hi).index(what)


def which(places, g, t):
    return [i for i, place in enumerate(places) if place == (g, t)]


def valid(h):
    return not isinstance(h, int) or 0 <= h < NH


def wait(eng, sem, value):
    if isinstance(value, int) and value <= 0:
        return
    eng.wait_ge(sem, value)


def all_steps(eng, step):
    def peeled(h):
        step(h, h % RING, h // RING, h)

    for h in range(FIRST, 3):
        peeled(h)
    with eng.Fori(0, 6) as it:
        for u in range(3, 3 + RING):
            step(it * RING + u, u % RING, it + u // RING, None)
    for h in range(27, LAST + 1):
        peeled(h)


def build(nc, x, wqkv, wlr, wg2, wo, wa, wb, onorm, br, rope, krows, cbias, identf, identb, tri,
          sel, hmean, out):
    q_parts = nc.dram_tensor("q_parts", (NH, NPART, HD, S), BF16, kind="Internal").ap()
    k_parts = nc.dram_tensor("k_parts", (NH, NPART, HD, KC), BF16, kind="Internal").ap()
    u_dram = nc.dram_tensor("u_dram", (NH, P, BW), F32, kind="Internal").ap()
    ew_dram = nc.dram_tensor("ew_dram", (NE, S), F32, kind="Internal").ap()
    xr = x.rearrange("a (n p) d -> p (a n) d", p=P)
    outr = out.rearrange("a (n p) d -> p (a n) d", p=P)

    with ExitStack() as ctx:
        def sb(name, shape, dt):
            return ctx.enter_context(nc.sbuf_tensor(name, shape, dt))

        def sem(name):
            return ctx.enter_context(nc.semaphore(name))

        ps = ctx.enter_context(nc.psum_tensor("ps", [P, 8, BW], F32))

        ARENA = 26700
        arena = sb("arena", [P, ARENA], F32)
        place = {"A": 0, "B": 0}

        def carve(stage, words):
            at = place[stage]
            place[stage] = at + words
            assert place[stage] <= ARENA, (stage, place)
            return arena[:, at:at + words]

        xnT = sb("xnT", [P, KT, S], F32)
        idf = sb("idf", [P, P], F32)
        idb = sb("idb", [P, P], BF16)
        tri_sb = sb("tri_sb", [P, P], BF16)
        cbias_sb = sb("cbias_sb", [P, QT, NC_], F32)
        lr = sb("lr", [P, BW], F32)
        vall = sb("vall", [P, NH * QT * VW], F32)
        v4 = vall[:].rearrange("p (h t w) -> p h t w", h=NH, t=QT)
        kstack = sb("kstack", [P, RING, KC], BF16)
        qstack = sb("qstack", [P, RING, S], BF16)
        w3 = carve("A", 3 * KT * D).rearrange("p (w k n) -> p w k n", w=3, k=KT)
        x_sb = vall[:, 0:8 * D].rearrange("p (t d) -> p t d", d=D)
        prod = carve("A", 8 * BW).rearrange("p (s k c) -> p s k c", s=2, k=4)
        rot = carve("A", 8 * BW).rearrange("p (s k c) -> p s k c", s=4, k=2)
        cs = carve("A", 2 * S).rearrange("p (k c) -> p k c", k=2)
        parts = carve("A", 4 * NPART * BW).bitcast(BF16).rearrange("p (s k a c) -> p s k a c", s=4, k=2, a=NPART)
        wlr_sb = carve("A", KT * 24).rearrange("p (k n) -> p k n", k=KT)
        ksum = carve("A", 2 * NC_).rearrange("p (k c) -> p k c", k=2)
        kmean = carve("A", 2 * NC_).rearrange("p (k c) -> p k c", k=2)
        kmp = carve("A", NPART * NC_).bitcast(BF16).rearrange("p (k a c) -> p k a c", k=2, a=NPART)
        stats = carve("A", 4 * 6).rearrange("p (t k) -> p t k", t=4)
        mv = carve("A", 4 * 2).rearrange("p (t k) -> p t k", t=4)
        rstd = carve("A", 4)
        LP = NE + 7
        lg = carve("A", QT * LP).rearrange("p (t e) -> p t e", t=QT)
        lghit = carve("A", QT * LP).rearrange("p (t e) -> p t e", t=QT)
        lmax8 = carve("A", QT * 8).rearrange("p (t e) -> p t e", t=QT)
        lexp = carve("A", QT * NE).rearrange("p (t e) -> p t e", t=QT)
        lsum = carve("A", QT)
        ew = carve("A", QT * NE).rearrange("p (t e) -> p t e", t=QT)
        ewT = carve("A", P)
        br_sb = carve("A", NE)
        prob = carve("B", 8 * BW).rearrange("p (s c) -> p s c", s=8)
        stage = carve("B", NB * BW).rearrange("p (b c) -> p b c", b=NB)
        vst = carve("B", 2 * QT * VW).rearrange("p (s t w) -> p s t w", s=2, t=QT)
        merged = carve("B", 2 * BW).rearrange("p (s c) -> p s c", s=2)
        GW = NC_ + TOPK
        graw = carve("B", QT * NC_).rearrange("p (t c) -> p t c", t=QT)
        gate = carve("B", QT * GW).rearrange("p (t c) -> p t c", t=QT)
        ghit = carve("B", QT * GW).rearrange("p (t c) -> p t c", t=QT)
        top8 = carve("B", QT * 8).rearrange("p (t e) -> p t e", t=QT)
        maskq = carve("B", QT * NC_ // 2).bitcast(BF16).rearrange("p (t c) -> p t c", t=QT)
        mxp = carve("B", 2 * QT * 4).rearrange("p (s t k) -> p s t k", s=2, t=QT)
        mx = carve("B", QT)
        nmax = carve("B", RING * P // 2).bitcast(BF16).rearrange("p (s c) -> p s c", s=RING)
        sel_sb = carve("B", VW)
        wo_sb = carve("B", KT * D).rearrange("p (k n) -> p k n", k=KT)
        wa_sb = carve("B", KT * D).rearrange("p (k n) -> p k n", k=KT)
        wb_sb = carve("B", KT * D).rearrange("p (k n) -> p k n", k=KT)
        wg2_sb = carve("B", D)
        hmean_sb = carve("B", P)
        onorm_sb = carve("B", 1)
        ewb = carve("B", 2 * KT * BW).rearrange("p (s k c) -> p s k c", s=2, k=KT)
        xres = carve("B", 4 * D).rearrange("p (t d) -> p t d", t=4)
        usq = carve("B", KT * BW).rearrange("p (k c) -> p k c", k=KT)
        u_sb = vall[:, 0:4096].rearrange("p (s k c) -> p s k c", s=2, k=KT)
        den = vall[:, 4096:8192].rearrange("p (s k c) -> p s k c", s=2, k=KT)
        sig = qstack[:].rearrange("p s c -> p (s c)").bitcast(F32).rearrange("p (s k c) -> p s k c", s=2, k=KT)
        hm = kstack[:].rearrange("p s c -> p (s c)").bitcast(F32)[:, 0:4096].rearrange("p (s k c) -> p s k c", s=2, k=KT)
        z = prob.rearrange("p (s k) c -> p s k c", s=2)
        osb = stage

        ld_x = [sem(f"ld_x{i}") for i in range(4)]
        ld_id = sem("ld_id")
        ld_wq = sem("ld_wq")
        ld_w = sem("ld_w")
        ld_v = sem("ld_v")
        ld_b = sem("ld_b")
        ld_k = sem("ld_k")
        ln_step = sem("ln_step")
        ln_sqrt = sem("ln_sqrt")
        ln_ready = sem("ln_ready")
        tp_done = sem("tp_done")
        tp_read = sem("tp_read")
        proj_done = sem("proj_done")
        proj_read = sem("proj_read")
        rot_done = sem("rot_done")
        hi_done = sem("hi_done")
        res_done = sem("res_done")
        mid_done = sem("mid_done")
        lo_done = sem("lo_done")
        ks_done = sem("ks_done")
        km_step = sem("km_step")
        st_part = [sem(f"st_part{i}") for i in range(4)]
        st_km = sem("st_km")
        v_done = sem("v_done")
        v_read = sem("v_read")
        ones_set = sem("ones_set")
        lr_done = sem("lr_done")
        lr_read = sem("lr_read")
        lgT_done = sem("lgT_done")
        rt_step = sem("rt_step")
        rt_exp = sem("rt_exp")
        ewT_done = sem("ewT_done")
        ewT_read = sem("ewT_read")
        st_ew = sem("st_ew")
        ps_clear = sem("ps_clear")
        b_init = sem("b_init")
        stage_clear = sem("stage_clear")
        ld_stack = [sem(f"ld_stack{i}") for i in range(RING)]
        ld_max = [sem(f"ld_max{i}") for i in range(RING)]
        s1_done = sem("s1_done")
        s1_read = sem("s1_read")
        s2_done = sem("s2_done")
        exp_done = sem("exp_done")
        tk_begun = sem("tk_begun")
        tri_begun = sem("tri_begun")
        tri_done = sem("tri_done")
        pv_done = sem("pv_done")
        pv_read = sem("pv_read")
        v_staged = sem("v_staged")
        gates_done = sem("gates_done")
        gates_biased = sem("gates_biased")
        misc_read = sem("misc_read")
        tk_step = sem("tk_step")
        mask_ready = sem("mask_ready")
        maskT_done = sem("maskT_done")
        mx_ready = sem("mx_ready")
        maxT_done = sem("maxT_done")
        merge_done = sem("merge_done")
        st_u = [sem(f"st_u{i}") for i in range(2)]
        ld_u = [sem(f"ld_u{i}") for i in range(2)]
        ld_ew = [sem(f"ld_ew{i}") for i in range(2)]
        ld_xr = sem("ld_xr")
        g_done = sem("g_done")
        sig_done = sem("sig_done")
        h_done = sem("h_done")
        hm_done = sem("hm_done")
        sq_done = sem("sq_done")
        l2_done = sem("l2_done")
        ms_done = sem("ms_done")
        sqrt_done = sem("sqrt_done")
        c_step = sem("c_step")
        den_read = sem("den_read")
        z_done = sem("z_done")
        o_done = sem("o_done")
        o_read = sem("o_read")
        st_o = [sem(f"st_o{i}") for i in range(4)]

        UNITS = [(g, n, w) for g in range(2) for n in range(NB) for w in range(2)]
        NU = len(UNITS)

        def pbank(u, half):
            return ps[:, 2 + (2 * u + half) % 4, :]

        S1 = [ps[:, b, :] for b in range(3)]
        S2 = [ps[:, 3 + b, :] for b in range(3)]
        PV = ps[:, 6, :]
        MISC = ps[:, 7, :]
        MISCB = MISC.bitcast(BF16)

        block = ctx.enter_context(nc.Block())

        @block.sync
        def _(sp):
            def load_x(b):
                sp.dma_start(x_sb[:, 4 * (b % 2):4 * (b % 2) + 4, :], xr[:, 4 * b:4 * b + 4, :]).then_inc(ld_x[b], 16)

            load_x(0)
            sp.dma_start(idf[:], identf).then_inc(ld_id, 16)
            sp.dma_start(w3[:, 0], wqkv[0]).then_inc(ld_wq, 16)
            load_x(1)
            sp.dma_start(cs, rope).then_inc(ld_w, 16)
            sp.dma_start(w3[:, 1], wqkv[1]).then_inc(ld_w, 16)
            for b in (2, 3):
                sp.wait_ge(tp_done, 4 * (b - 1))
                load_x(b)
            sp.dma_start(wlr_sb, wlr).then_inc(ld_v, 16)
            sp.dma_start(br_sb, br.partition_broadcast(P)).then_inc(ld_v, 16)
            sp.dma_start(w3[:, 2], wqkv[2]).then_inc(ld_v, 16)
            for s in range(RING):
                sp.dma_start(kstack[96:128, s, 0:S], krows).then_inc(ld_k, 16)
            sp.dma_start(idb[:], identb).then_inc(ld_k, 16)
            sp.dma_start(tri_sb[:], tri).then_inc(ld_k, 16)
            sp.dma_start(cbias_sb[:], cbias).then_inc(ld_k, 16)

            def load_stack(h, s):
                q, k = q_parts[bass.ds(h, 1)], k_parts[bass.ds(h, 1)]
                for dst, src in (
                        (kstack[0:48, s, :], k[:, 0].broadcast_to((3, HD, KC))),
                        (kstack[48:80, s, :], k[:, 1].broadcast_to((2, HD, KC))),
                        (kstack[80:96, s, :], k[:, 2]),
                        (qstack[0:48, s, :], q[:, 0:3]),
                        (qstack[48:80, s, :], q[:, 0:2]),
                        (qstack[80:96, s, :], q[:, 0])):
                    sp.dma_start(dst, src).then_inc(ld_stack[s], 16)

            for u, (g, n, w) in enumerate(UNITS):
                sp.wait_ge(lo_done, u + 1)
                dst = (q_parts, k_parts)[w]
                for half in range(2):
                    for a in range(NPART):
                        sp.dma_start(
                            dst[16 * g:16 * g + 16, a, HH * half:HH * half + HH, n * BW:(n + 1) * BW],
                            parts[:, u % 4, half, a, :]).then_inc(st_part[u % 4], 16)
                if w == 1 and n == NB - 1:
                    sp.wait_ge(km_step, 6 * (g + 1))
                    for half in range(2):
                        for a in range(NPART):
                            sp.dma_start(
                                k_parts[16 * g:16 * g + 16, a, HH * half:HH * half + HH, S:KC],
                                kmp[:, half, a, :]).then_inc(st_km, 16)
                    for s in range(4):
                        sp.wait_ge(st_part[s], 96 * NU // 8 * (g + 1))
                    sp.wait_ge(st_km, 96 * (g + 1))
                    if g == 0:
                        load_stack(0, 0)
                if u == NU - 3:
                    sp.wait_ge(ewT_read, 1)
                    sp.dma_start(ew_dram.rearrange("e (t c) -> t e c", t=QT), ewT).then_inc(st_ew, 16)
            sp.wait_ge(st_ew, 16)

            def load_ew(n):
                for m in range(KT):
                    sp.dma_start(ewb[:, n % 2, m, :], ew_dram[2 * m:2 * m + 2, n * BW:(n + 1) * BW].unsqueeze(1)
                                 .broadcast_to((2, RANK, BW))).then_inc(ld_ew[n % 2], 16)

            def step(h, hs, hq, hi):
                ahead = h + 3
                if valid(ahead) and hi != FIRST:
                    wait(sp, s2_done, NP_ * h)
                    load_stack(ahead, (hs + 3) % RING)
                if hi == 0:
                    sp.wait_ge(v_read, QT)
                    sp.wait_ge(stage_clear, 1)
                    for dst, src in ((sel_sb, sel), (wo_sb, wo), (wa_sb, wa), (wb_sb, wb), (hmean_sb, hmean)):
                        sp.dma_start(dst, src).then_inc(ld_b, 16)
                    for b in range(NB):
                        sp.dma_start(wg2_sb[32 * b:32 * b + 16, :], wg2).then_inc(ld_b, 16)
                    for g in range(8):
                        sp.dma_start(onorm_sb[16 * g:16 * g + 16, :], onorm).then_inc(ld_b, 16)
                    load_ew(0)
                    load_ew(1)
                if valid(h - 1):
                    sp.wait_ge(misc_read, misc_count(h, hi, "merge") + 1)
                    sp.dma_start(u_dram[bass.ds(h - 1, 1)], merged[:, (hs - 1) % 2, :]).then_inc(st_u[(hs - 1) % 2], 16)
                if valid(h + 1):
                    sp.wait_ge(misc_read, misc_count(h, hi, "max") + 1)
                    s = (hs + 1) % RING
                    sp.dma_start(qstack[127:128, s, :], nmax[0:QT, s, :]).then_inc(ld_max[s], 16)

            all_steps(sp, step)

            def load_u(n):
                for j in range(KT):
                    src = u_dram[8 * j:8 * j + 8]
                    sp.dma_start(u_sb[:, n % 2, j, :], src[:, 32 * n:32 * n + HD, :]).then_inc(ld_u[n % 2], 16)
                    sp.dma_start(den[:, n % 2, j, :], src[:, 32 * n + HD:32 * n + HD + 1, :]
                                 .broadcast_to((8, HD, BW))).then_inc(ld_u[n % 2], 16)

            def load_res(n):
                sp.dma_start(xres, xr[:, 4 * n:4 * n + 4, :]).then_inc(ld_xr, 16)

            for s in range(2):
                sp.wait_ge(st_u[s], 16 * NH // 2)
            load_u(0)
            load_u(1)
            load_res(0)
            for n in range(NB):
                if n + 2 < NB:
                    sp.wait_ge(z_done, KT * (n + 1))
                    load_u(n + 2)
                    sp.wait_ge(hm_done, KT * (n + 1))
                    load_ew(n + 2)
                for t in range(4 * n, 4 * n + 4):
                    sp.wait_ge(o_read, t + 1)
                    sp.dma_start(outr[:, t, :], osb[:, t % 4, :]).then_inc(st_o[t % 4], 16)
                if n + 1 < NB:
                    load_res(n + 1)
            for t in range(4):
                sp.wait_ge(st_o[t], 16 * NB)

        @block.tensor
        def _(pe):
            pe.wait_ge(ld_id, 16)
            pe.wait_ge(ps_clear, 1)

            def turn_block(b):
                pe.wait_ge(ln_ready, 4 * (b + 1))
                for k in range(KT):
                    n = 4 * b + k
                    wait(pe, tp_read, n - 1)
                    for t in range(4):
                        mm = pe.transpose(ps[:, n % 2, t * P:(t + 1) * P], x_sb[:, 4 * (b % 2) + t, k * P:(k + 1) * P],
                                          idf[:])
                    mm.then_inc(tp_done, 1)

            def project(u):
                g, n, w = UNITS[u]
                pe.wait_ge(tp_read, 4 * (n + 1))
                wait(pe, proj_read, u - 1)
                for half in range(2):
                    for k in range(KT):
                        m = 2 * g + half
                        mm = pe.matmul(pbank(u, half), w3[:, w, k, m * P:(m + 1) * P], xnT[:, k, n * BW:(n + 1) * BW],
                                       start=(k == 0), stop=(k == KT - 1))
                mm.then_inc(proj_done, 1)

            turn_block(0)
            for u in range(NU):
                if u == 0:
                    pe.wait_ge(ld_wq, 16)
                if u == 1:
                    pe.wait_ge(ld_w, 16 * 2)
                if u % 2 == 0 and u // 2 + 1 < NB:
                    turn_block(u // 2 + 1)
                project(u)
                if u == 7:
                    pe.wait_ge(ld_v, 16 * 3)
                    for k in range(KT):
                        for n in range(NB):
                            mm = pe.matmul(ps[32 * n:32 * n + 24, 6, :], wlr_sb[:, k, :], xnT[:, k, n * BW:(n + 1) * BW],
                                           start=(k == 0), stop=(k == KT - 1), tile_position=(0, 32 * n))
                    mm.then_inc(lr_done, 1)
                if u == 8:
                    pe.wait_ge(lr_read, 1)
                    for s in range(4):
                        mm = pe.transpose(MISC[:, s * P:(s + 1) * P], lr[:, s * P:(s + 1) * P], idf[:])
                    mm.then_inc(lgT_done, 1)
                if u == 12:
                    pe.wait_ge(rt_step, 7)
                    pe.transpose(ps[:, 6, 0:P], ew.rearrange("p t e -> p (t e)"), idf[:]).then_inc(ewT_done, 1)

            def v_tile(t):
                wait(pe, v_read, t - 3)
                for k in range(KT):
                    mm = pe.matmul(ps[:, 3 + t % 4, :], xnT[:, k, t * P:(t + 1) * P], w3[:, 2, k, :],
                                   start=(k == 0), stop=(k == KT - 1))
                mm.then_inc(v_done, 1)

            pe.wait_ge(proj_read, NU)
            pe.wait_ge(ewT_read, 1)

            def piece(h, hs, n):
                i, p = PIECES[n]
                s, bank = hs % RING, S1[BANK[n]]
                wait(pe, s1_read, NP_ * h + (n - bank_before(n) + 1))
                last = p == i // 4
                w = (i % 4 + 1) * P if last else BW
                mm = pe.matmul(bank[:, 0:w], qstack[0:127, s, i * P:(i + 1) * P], kstack[0:127, s, p * BW:p * BW + w],
                               start=True, stop=not last)
                if last:
                    mm = pe.matmul(bank[:, w - P:w], idb[:], tri_sb[:], start=False, stop=True)
                mm.then_inc(s1_done, 1)

            def tile(h, hs, n):
                b, j = TILES[n]
                s, r = hs % RING, max(0, j - 4 * b)
                wait(pe, exp_done, NP_ * h + (n - bank_before(n) + 1))
                w = BW - r * P
                pe.matmul(S2[BANK[n]][:, 0:w], kstack[:, s, j * P:(j + 1) * P], qstack[:, s, b * BW + r * P:(b + 1) * BW],
                          start=True, stop=True).then_inc(s2_done, 1)

            def values(h, hs, g):
                b = TILES[4 * g][0]
                if g == 0:
                    pe.wait_ge(v_staged, h + 1)
                pe.wait_ge(exp_done, NP_ * h + 4 * (g + 1))
                if g in LAST_GROUP:
                    pe.wait_ge(tri_done, QT * h + 4 * (b + 1))
                if TILES[4 * g][1] == 0:
                    wait(pe, pv_read, NB * h + b)
                for t in range(4):
                    n = 4 * g + t
                    j = TILES[n][1]
                    r = max(0, j - 4 * b)
                    mm = pe.matmul(PV[32 * t:32 * t + VW, r * P:BW], vst[:, hs % 2, j, :],
                                   prob[:, n % 8, 0:BW - r * P], start=(j < 4), stop=(g in LAST_GROUP),
                                   tile_position=(0, 32 * t))
                mm.then_inc(pv_done, 1)

            def expert_product(n, m, k):
                q = 4 * n + m
                if k == 0:
                    wait(pe, hm_done, q - 1)
                mm = pe.matmul(ps[:, q % 2, :], wa_sb[:, k, m * P:(m + 1) * P], xnT[:, k, n * BW:(n + 1) * BW],
                               start=(k == 0), stop=(k == KT - 1))
                if k == KT - 1:
                    mm.then_inc(h_done, 1)

            def step(h, hs, hq, hi):

                def turn(off):
                    return hq + (hs + off) // RING + 1

                if hi == 0:
                    pe.wait_ge(v_read, QT)
                if hi == 1:
                    pe.wait_ge(ld_b, 16 * 17)
                for g in range(NG):
                    ahead = (g + LEAD) // NG + 1
                    for t in range(4):
                        if valid(h + ahead):
                            n = 4 * ((g + LEAD) % NG) + t
                            if n == 0:
                                pe.wait_ge(misc_read, misc_count(h, hi, "mask0") + 1)
                            if PIECES[n] == (QT // 2, 0):
                                lastly = None if hi is None or hi >= 2 else hi - 1
                                pe.wait_ge(misc_read, misc_count(h - 1, lastly, "mask1") + 1)
                            piece(h + ahead, hs + ahead, n)
                        if valid(h):
                            n = 4 * g + t
                            if n == 0:
                                pe.wait_ge(ld_max[hs % RING], 16 * turn(0))
                            tile(h, hs, n)
                        if hi == NH - 1 and t == 1:
                            if g == 0:
                                pe.wait_ge(s1_read, NP_ * NH)
                            expert_product(0, g // KT, g % KT)
                        if (g, t) == MAX_AT and valid(h + 1):
                            pe.wait_ge(mx_ready, h + 2)
                            wait(pe, misc_read, misc_count(h, hi, "max"))
                            pe.transpose(MISC[0:QT, 0:P], mx, idf[:]).then_inc(maxT_done, 1)
                    if g > 0 and valid(h):
                        values(h, hs, g - 1)
                    if g == 0 and valid(h - 1):
                        values(h - 1, hs - 1, NG - 1)
                    if (hi, g) in V_AT:
                        v_tile(V_AT.index((hi, g)))
                    if g == 1 and valid(h - 1):
                        pe.wait_ge(pv_read, NB * h)
                        wait(pe, misc_read, misc_count(h, hi, "merge"))
                        for b in range(NB):
                            mm = pe.matmul(MISC[32 * b:32 * b + VW, :], sel_sb, stage[:, b, :],
                                           start=True, stop=True, tile_position=(0, 32 * b))
                        mm.then_inc(merge_done, 1)
                    if g in MASKS_AT and valid(h + 2):
                        half = MASKS_AT.index(g)
                        if half == 0:
                            pe.wait_ge(mask_ready, h + 3)
                        wait(pe, misc_read, misc_count(h, hi, f"mask{half}"))
                        for i in range(QT // 2):
                            mm = pe.transpose(MISCB[96:128, i * P:(i + 1) * P], maskq[:, half * QT // 2 + i, :],
                                              idb[:], tile_position=(0, 96))
                        mm.then_inc(maskT_done, 1)
                    if g == GATES_AT and valid(h + 3):
                        s = (hs + 3) % RING
                        if hi == FIRST:
                            pe.wait_ge(ld_k, 16 * (RING + 3))
                        pe.wait_ge(ld_stack[s], 96 * turn(3))
                        wait(pe, misc_read, misc_count(h, hi, "gates"))
                        for i in range(QT):
                            mm = pe.matmul(MISC[:, i * NC_:(i + 1) * NC_], qstack[0:96, s, i * P:(i + 1) * P],
                                           kstack[0:96, s, S:KC], start=True, stop=True)
                        mm.then_inc(gates_done, 1)

            all_steps(pe, step)

            pe.wait_ge(exp_done, NP_ * NH)
            pe.wait_ge(pv_read, NB * NH)
            pe.wait_ge(misc_read, misc_count(LAST, LAST, "merge") + 1)

            def output(n):
                pe.wait_ge(z_done, KT * (n + 1))
                for t in range(4):
                    q = 4 * n + t
                    wait(pe, o_read, q - 1)
                    for k in range(KT):
                        pe.matmul(ps[:, 6 + q % 2, :], hm[:, n % 2, k, t * P:(t + 1) * P], wb_sb[:, k, :],
                                  start=(k == 0), stop=False)
                    for k in range(KT):
                        mm = pe.matmul(ps[:, 6 + q % 2, :], z[:, n % 2, k, t * P:(t + 1) * P], wo_sb[:, k, :],
                                       start=False, stop=(k == KT - 1))
                    mm.then_inc(o_done, 1)

            for n in range(NB):
                for j in range(KT):
                    q = 4 * n + j
                    wait(pe, sig_done, q - 1)
                    pe.matmul(ps[:, 2 + q % 2, :], wg2_sb[32 * n:32 * n + 16, j * P:(j + 1) * P], lr[32 * n:32 * n + 16, :],
                              start=True, stop=True, tile_position=(32 * n, 0)).then_inc(g_done, 1)
                    for k in range(KT):
                        if KT * q + k >= NG:
                            expert_product(n, j, k)
                for j in range(KT):
                    q = 4 * n + j
                    pe.wait_ge(sq_done, q + 1)
                    wait(pe, den_read, q - 1)
                    pe.matmul(ps[:, 4 + q % 2, :], hmean_sb, usq[:, j, :], start=True, stop=True).then_inc(ms_done, 1)
                if n >= 1:
                    output(n - 1)
            output(NB - 1)

        @block.scalar
        def _(act):
            def deviations(b):
                act.wait_ge(ln_step, 4 * b + 3)
                nc.scalar.activation(rstd, rstd, ACT.Sqrt).then_inc(ln_sqrt, 1)

            def turn_block(b):
                for k in range(KT):
                    n = 4 * b + k
                    act.wait_ge(tp_done, n + 1)
                    nc.scalar.copy(xnT[:, k, b * BW:(b + 1) * BW], ps[:, n % 2, :]).then_inc(tp_read, 1)

            deviations(0)
            deviations(1)
            turn_block(0)
            for u in range(NU + 1):
                if u == 0:
                    turn_block(1)
                    deviations(2)
                if u == 1:
                    deviations(3)
                if u in (1, 3):
                    turn_block((u + 3) // 2)
                if u < NU:
                    act.wait_ge(rot_done, u + 1)
                    if u >= 4:
                        act.wait_ge(st_part[u % 4], 96 * (u // 4))
                    nc.scalar.copy(parts[:, u % 4, :, 0, :], rot[:, u % 4]).then_inc(hi_done, 1)
                if u >= 1:
                    act.wait_ge(res_done, u)
                    nc.scalar.copy(parts[:, (u - 1) % 4, :, 1, :], rot[:, (u - 1) % 4]).then_inc(mid_done, 1)
                if u == 7:
                    act.wait_ge(lr_done, 1)
                    nc.scalar.copy(lr[:], ps[:, 6, :]).then_inc(lr_read, 1)
                if u == 10:
                    act.wait_ge(rt_step, 3)
                    nc.scalar.activation(lexp, lexp, ACT.Exp).then_inc(rt_exp, 1)
                if u == 12:
                    act.wait_ge(ewT_done, 1)
                    nc.scalar.copy(ewT, ps[:, 6, 0:P]).then_inc(ewT_read, 1)

            def v_copy(t):
                if t == 0:
                    act.wait_ge(ones_set, 1)
                act.wait_ge(v_done, t + 1)
                nc.scalar.copy(v4[:, :, t, 0:HD], ps[:, 3 + t % 4, :].rearrange("p (h d) -> p h d", h=NH)).then_inc(v_read, 1)

            def evac(h, b, g):
                act.wait_ge(pv_done, NG * h + g + 1)
                if b == 0:
                    wait(act, merge_done, h)
                    if isinstance(h, int) and h == 0:
                        act.wait_ge(stage_clear, 1)
                    for r in range(4):
                        cp = nc.scalar.copy(stage[0:32 * (r + 1), 0, r * P:(r + 1) * P],
                                            PV[0:32 * (r + 1), r * P:(r + 1) * P])
                else:
                    cp = nc.scalar.copy(stage[:, b, :], PV)
                cp.then_inc(pv_read, 1)

            def step(h, hs, hq, hi):
                for g in range(NG):
                    for t in range(4):
                        if (g, t) == (2, 2) and valid(h - 1):
                            act.wait_ge(merge_done, h)
                            if hi is None or hi >= 3:
                                act.wait_ge(st_u[(hs - 1) % 2], (hq * 2 + (hs - 1) // 2) * 16)
                            nc.scalar.copy(merged[:, (hs - 1) % 2, :], MISC).then_inc(misc_read, 1)
                        if t in (0, 2) and g - 1 in MASKS_AT and valid(h + 2):
                            half, quarter = MASKS_AT.index(g - 1), t // 2
                            if quarter == 0:
                                act.wait_ge(maskT_done, 2 * (h + 2) + half + 1)
                            at = half * S // 2 + quarter * S // 4
                            cp = nc.scalar.copy(qstack[96:128, (hs + 2) % RING, at:at + S // 4],
                                                MISCB[96:128, quarter * S // 4:(quarter + 1) * S // 4])
                            if quarter == 1:
                                cp.then_inc(misc_read, 1)
                        if t == 0 and g - 1 == GATES_AT and valid(h + 3):
                            act.wait_ge(gates_done, h + 4)
                            if hi == FIRST:
                                act.wait_ge(b_init, 1)
                            wait(act, gates_biased, h + 3)
                            nc.scalar.copy(graw, MISC.rearrange("p (t c) -> p t c", t=QT)).then_inc(misc_read, 1)
                        if t == 2 and g == MAX_AT[0] and valid(h + 1):
                            act.wait_ge(maxT_done, h + 2)
                            nc.scalar.mul(nmax[0:QT, (hs + 1) % RING, :], MISC[0:QT, 0:P], -1.0).then_inc(misc_read, 1)
                        if not valid(h):
                            continue
                        n = 4 * g + t
                        b, j = TILES[n]
                        w = BW - max(0, j - 4 * b) * P
                        if t == 0:
                            wait(act, pv_done, NG * h + (g - 1))
                        act.wait_ge(s2_done, NP_ * h + n + 1)
                        nc.scalar.activation(prob[:, n % 8, 0:w], S2[BANK[n]][:, 0:w], ACT.Exp,
                                             scale=float(HD) ** -0.5).then_inc(exp_done, 1)
                    if (hi, g) in V_AT:
                        v_copy(V_AT.index((hi, g)))
                    if g == 0 and valid(h - 1):
                        evac(h - 1, NB - 1, NG - 1)
                    if g in EVAC_AT and valid(h):
                        evac(h, EVAC_AT.index(g), list(LAST_GROUP)[EVAC_AT.index(g)])

            all_steps(act, step)

            for n in range(NB):
                wait(act, z_done, KT * (n - 1))
                for j in range(KT):
                    q = 4 * n + j
                    act.wait_ge(g_done, q + 1)
                    nc.scalar.activation(sig[:, n % 2, j, :], ps[:, 2 + q % 2, :], ACT.Sigmoid).then_inc(sig_done, 1)
                act.wait_ge(ld_u[n % 2], 128 * (n // 2 + 1))
                wait(act, ms_done, KT * n)
                for j in range(KT):
                    nc.scalar.activation(usq[:, j, :], u_sb[:, n % 2, j, :], ACT.Square).then_inc(sq_done, 1)
                for j in range(KT):
                    nc.scalar.activation(den[:, n % 2, j, :], den[:, n % 2, j, :], ACT.Square,
                                         scale=RMS_EPS ** 0.5).then_inc(l2_done, 1)
                for j in range(KT):
                    q = 4 * n + j
                    act.wait_ge(den_read, q + 1)
                    nc.scalar.activation(den[:, n % 2, j, :], den[:, n % 2, j, :], ACT.Sqrt).then_inc(sqrt_done, 1)

        @block.vector
        def _(dve):
            nc.vector.memset(ps[:], 0.0).then_inc(ps_clear, 1)
            def statistics(b):
                dve.wait_ge(ld_x[b], 16)
                sl, links = 4 * (b % 2), 4 * b
                for t in range(4):
                    cp = nc.vector.bn_stats(stats[:, t, :], x_sb[:, sl + t, :])
                cp.then_inc(ln_step, 1)
                dve.wait_ge(ln_step, links + 1)
                for t in range(4):
                    cp = nc.vector.bn_aggr(mv[:, t, :], stats[:, t, :])
                cp.then_inc(ln_step, 1)
                dve.wait_ge(ln_step, links + 2)
                nc.vector.tensor_scalar(rstd, mv[:, :, 1], LN_EPS, None, ALU.add).then_inc(ln_step, 1)

            def normalise(b):
                sl, links = 4 * (b % 2), 4 * b
                dve.wait_ge(ln_sqrt, b + 1)
                nc.vector.reciprocal(rstd, rstd).then_inc(ln_step, 1)
                dve.wait_ge(ln_step, links + 4)
                for t in range(4):
                    nc.vector.tensor_scalar(x_sb[:, sl + t, :], x_sb[:, sl + t, :], mv[:, t, 0:1], rstd[:, t:t + 1],
                                            ALU.subtract, ALU.mult).then_inc(ln_ready, 1)

            def mean_keys(g):
                base = 6 * g
                if g:
                    dve.wait_ge(st_km, 96)
                dve.wait_ge(res_done, 8 * g + 8)
                nc.vector.tensor_scalar(kmean, ksum, 1.0 / CH, None, ALU.mult).then_inc(km_step, 1)
                dve.wait_ge(km_step, base + 1)
                nc.vector.tensor_copy(kmp[:, :, 0, :], kmean).then_inc(km_step, 1)
                dve.wait_ge(km_step, base + 2)
                nc.vector.tensor_tensor(kmean, kmean, kmp[:, :, 0, :], ALU.subtract).then_inc(km_step, 1)
                dve.wait_ge(km_step, base + 3)
                nc.vector.tensor_copy(kmp[:, :, 1, :], kmean).then_inc(km_step, 1)
                dve.wait_ge(km_step, base + 4)
                nc.vector.tensor_tensor(kmean, kmean, kmp[:, :, 1, :], ALU.subtract).then_inc(km_step, 1)
                dve.wait_ge(km_step, base + 5)
                nc.vector.tensor_copy(kmp[:, :, 2, :], kmean).then_inc(km_step, 1)

            def route(part):
                if part == 0:
                    nc.vector.memset(lg[:, :, NE:LP], SENT)
                    nc.vector.memset(lmax8, SENT)
                    dve.wait_ge(ld_v, 16 * 3)
                    dve.wait_ge(lgT_done, 1)
                    nc.vector.tensor_tensor(
                        lg[:, :, 0:NE].rearrange("p (q s) e -> p q s e", q=4),
                        MISC.rearrange("p (s q r) -> p q s r", s=4, q=4)[:, :, :, 16:16 + NE],
                        br_sb.unsqueeze(1).unsqueeze(1).broadcast_to((P, 4, 4, NE)), ALU.add).then_inc(rt_step, 1)
                    dve.wait_ge(rt_step, 1)
                    nc.vector.tensor_reduce(lmax8[:, :, 0:1], lg[:, :, 0:NE], AX.X, ALU.max).then_inc(rt_step, 1)
                    dve.wait_ge(rt_step, 2)
                    for t in range(QT):
                        nc.vector.match_replace(lghit[:, t, :], lmax8[:, t, :], lg[:, t, :], HIT)
                    nc.vector.tensor_tensor(lexp, lg[:, :, 0:NE], lmax8[:, :, 0:1].broadcast_to((P, QT, NE)),
                                            ALU.subtract).then_inc(rt_step, 1)
                if part == 1:
                    dve.wait_ge(rt_exp, 1)
                    nc.vector.tensor_reduce(lsum, lexp, AX.X, ALU.add).then_inc(rt_step, 1)
                    dve.wait_ge(rt_step, 4)
                    nc.vector.tensor_scalar(lsum, lsum, float(RANK), None, ALU.mult).then_inc(rt_step, 1)
                    dve.wait_ge(rt_step, 5)
                    nc.vector.reciprocal(lsum, lsum).then_inc(rt_step, 1)
                    dve.wait_ge(rt_step, 6)
                    nc.vector.scalar_tensor_tensor(out=ew, in0=lghit[:, :, 0:NE], scalar=HIT,
                                                   in1=lsum.unsqueeze(2).broadcast_to((P, QT, NE)),
                                                   op0=ALU.is_equal, op1=ALU.mult).then_inc(rt_step, 1)

            for b in range(2):
                statistics(b)
                normalise(b)
            statistics(2)
            normalise(2)
            dve.wait_ge(ld_w, 16 * 2)
            for u in range(NU + 2):
                if u == 1:
                    statistics(3)
                if u == 10:
                    route(0)
                if u == 12:
                    route(1)
                if u < NU:
                    n = UNITS[u][1]
                    dve.wait_ge(proj_done, u + 1)
                    wait(dve, rot_done, u - 1)
                    lo, hi = pbank(u, 0), pbank(u, 1)
                    cos, sin = cs[:, 0, n * BW:(n + 1) * BW], cs[:, 1, n * BW:(n + 1) * BW]
                    nc.vector.tensor_tensor(prod[:, u % 2, 0], lo, cos, ALU.mult)
                    nc.vector.tensor_tensor(prod[:, u % 2, 1], hi, sin, ALU.mult)
                    nc.vector.tensor_tensor(prod[:, u % 2, 2], lo, sin, ALU.mult)
                    nc.vector.tensor_tensor(prod[:, u % 2, 3], hi, cos, ALU.mult).then_inc(proj_read, 1)
                if u == 1:
                    normalise(3)
                if 1 <= u <= NU:
                    v = u - 1
                    g, n, w = UNITS[v]
                    dve.wait_ge(hi_done, v + 1)
                    if w == 1:
                        if n == 0 and g:
                            dve.wait_ge(km_step, 6 * g)
                        nc.vector.tensor_reduce(ksum[:, :, 8 * n:8 * n + 8],
                                                rot[:, v % 4].rearrange("p a (c k) -> p a c k", k=CH), AX.X,
                                                ALU.add).then_inc(ks_done, 1)
                        dve.wait_ge(ks_done, NB * g + n + 1)
                    nc.vector.tensor_tensor(rot[:, v % 4], rot[:, v % 4], parts[:, v % 4, :, 0, :],
                                            ALU.subtract).then_inc(res_done, 1)
                if u >= 2:
                    v = u - 2
                    g, n, w = UNITS[v]
                    dve.wait_ge(mid_done, v + 1)
                    nc.vector.tensor_tensor(parts[:, v % 4, :, 2, :], rot[:, v % 4], parts[:, v % 4, :, 1, :],
                                            ALU.subtract).then_inc(lo_done, 1)
                    if w == 1 and n == NB - 1:
                        mean_keys(g)
            for s in range(4):
                dve.wait_ge(st_part[s], 96 * NU // 4)
            dve.wait_ge(st_km, 192)
            nc.vector.memset(mxp, -SENT)
            nc.vector.memset(gate[:, :, NC_:GW], SENT).then_inc(b_init, 1)
            dve.wait_ge(b_init, 1)

            def step(h, hs, hq, hi):
                if hi == 0:
                    dve.wait_ge(v_done, QT)
                    nc.vector.memset(stage[:, 0, :], 0.0).then_inc(stage_clear, 1)
                for g in range(NG):
                    ahead = (g + LEAD) // NG + 1
                    links = 3 * (h + 2)
                    if g == CLEAR_AT and valid(h + 2):
                        dve.wait_ge(tk_step, links + 1)
                        nc.vector.memset(top8[:, :, TOPK:8], SENT).then_inc(tk_step, 1)
                    for t in range(4):
                        if (g, t) in TOP_AT and valid(h + 3):
                            if (g, t) == TOP_AT[0]:
                                dve.wait_ge(gates_biased, h + 4)
                                dve.sem_inc(tk_begun, 1)
                            for i in which(TOP_AT, g, t):
                                cp = nc.vector.max(top8[:, i, :], gate[:, i, 0:NC_])
                            if (g, t) == TOP_AT[-1]:
                                cp.then_inc(tk_step, 1)
                        if (g, t) in MATCH_AT and valid(h + 2):
                            if (g, t) == MATCH_AT[0]:
                                dve.wait_ge(tk_step, links + 2)
                                dve.sem_inc(tk_begun, 1)
                            for i in which(MATCH_AT, g, t):
                                cp = nc.vector.match_replace(ghit[:, i, :], top8[:, i, :], gate[:, i, :], HIT)
                            if (g, t) == MATCH_AT[-1]:
                                cp.then_inc(tk_step, 1)
                        if valid(h + ahead):
                            n = 4 * ((g + LEAD) % NG) + t
                            i, p = PIECES[n]
                            w = (i % 4 + 1) * P if p == i // 4 else BW
                            dve.wait_ge(s1_done, NP_ * (h + ahead) + n + 1)
                            nc.vector.tensor_reduce(mxp[:, (hs + ahead) % 2, i, p:p + 1], S1[BANK[n]][:, 0:w], AX.X,
                                                    ALU.max).then_inc(s1_read, 1)
                    if g == NG - 1 - LEAD and valid(h + 1):
                        dve.wait_ge(s1_read, NP_ * (h + 2))
                        wait(dve, maxT_done, h + 1)
                        nc.vector.tensor_reduce(mx, mxp[:, (hs + 1) % 2], AX.X, ALU.max).then_inc(mx_ready, 1)
                    if g == 3 and valid(h + 2):
                        dve.wait_ge(tk_step, links + 3)
                        wait(dve, maskT_done, 2 * (h + 2))
                        nc.vector.tensor_scalar(maskq, ghit[:, :, 0:NC_], HIT, MASK, ALU.not_equal,
                                                ALU.mult).then_inc(mask_ready, 1)

            all_steps(dve, step)

            def add_residual(n, t):
                q = 4 * n + t
                if t == 0:
                    dve.wait_ge(ld_xr, 16 * (n + 1))
                if n >= 1:
                    dve.wait_ge(st_o[t], 16 * n)
                dve.wait_ge(o_done, q + 1)
                nc.vector.tensor_tensor(osb[:, t, :], ps[:, 6 + q % 2, :], xres[:, t, :], ALU.add).then_inc(o_read, 1)

            def weigh(n, m):
                q = 4 * n + m
                if m == 0:
                    dve.wait_ge(ld_ew[n % 2], 64 * (n // 2 + 1))
                    wait(dve, o_done, 4 * (n - 1))
                dve.wait_ge(h_done, q + 1)
                nc.vector.tensor_tensor(hm[:, n % 2, m, :], ps[:, q % 2, :], ewb[:, n % 2, m, :], ALU.mult).then_inc(hm_done, 1)

            for n in range(NB):
                s = n % 2
                if n != 1:
                    for m in range(KT):
                        weigh(n, m)
                for j in range(KT):
                    q = 4 * n + j
                    dve.wait_ge(ms_done, q + 1)
                    dve.wait_ge(l2_done, q + 1)
                    nc.vector.tensor_tensor(den[:, s, j, :], ps[:, 4 + q % 2, :], den[:, s, j, :], ALU.add).then_inc(den_read, 1)
                for j in range(KT):
                    q = 4 * n + j
                    dve.wait_ge(sqrt_done, q + 1)
                    nc.vector.reciprocal(den[:, s, j, :], den[:, s, j, :]).then_inc(c_step, 1)
                    dve.wait_ge(c_step, 2 * q + 1)
                    nc.vector.tensor_tensor(den[:, s, j, :], den[:, s, j, :], u_sb[:, s, j, :], ALU.mult).then_inc(c_step, 1)
                    dve.wait_ge(c_step, 2 * q + 2)
                    dve.wait_ge(sig_done, q + 1)
                    nc.vector.scalar_tensor_tensor(out=z[:, s, j, :], in0=den[:, s, j, :], scalar=onorm_sb, in1=sig[:, s, j, :],
                                                   op0=ALU.mult, op1=ALU.mult).then_inc(z_done, 1)
                    if n == 0:
                        weigh(1, j)
                    else:
                        add_residual(n - 1, j)
            for t in range(4):
                add_residual(NB - 1, t)

        @block.gpsimd
        def _(pool):
            for u in range(NU):
                pool.wait_ge(proj_read, u + 1)
                wait(pool, lo_done, u - 3)
                nc.gpsimd.tensor_tensor(rot[:, u % 4, 0], prod[:, u % 2, 0], prod[:, u % 2, 1], ALU.subtract)
                nc.gpsimd.tensor_tensor(rot[:, u % 4, 1], prod[:, u % 2, 2], prod[:, u % 2, 3], ALU.add).then_inc(rot_done, 1)
            pool.wait_ge(tp_done, 4 * NB)
            nc.gpsimd.memset(v4[:, :, :, HD:VW], 1.0).then_inc(ones_set, 1)
            pool.wait_ge(b_init, 1)
            pool.wait_ge(ld_k, 16 * (RING + 3))

            def step(h, hs, hq, hi):
                for g in range(NG):
                    if g == 5 and valid(h + 1):
                        if hi == -1:
                            pool.wait_ge(v_read, QT)
                        wait(pool, pv_done, NG * h)
                        nc.gpsimd.tensor_copy(vst[:, (hs + 1) % 2].rearrange("p t w -> p (t w)"),
                                              vall[:].rearrange("p (h w) -> p h w", h=NH)[:, bass.ds(h + 1, 1), :]
                                              .rearrange("p h w -> p (h w)")).then_inc(v_staged, 1)
                    for t in range(4 * valid(h)):
                        n = 4 * g + t
                        b, j = TILES[n]
                        if j >= 4 * b:
                            pool.wait_ge(exp_done, NP_ * h + n + 1)
                            pool.sem_inc(tri_begun, 1)
                            pb = prob[:, n % 8, 0:P]
                            nc.gpsimd.affine_select(out=pb, in_=pb, compare_op=ALU.is_ge, fill=0.0, base=0,
                                                    pattern=[[1, P]], channel_multiplier=-1).then_inc(tri_done, 1)
                    if g - 2 == GATES_AT and valid(h + 3):
                        wait(pool, tk_step, 3 * (h + 3))
                        pool.wait_ge(misc_read, misc_count(h, hi, "gates") + 1)
                        nc.gpsimd.tensor_tensor(gate[:, :, 0:NC_], graw, cbias_sb[:], ALU.add).then_inc(gates_biased, 1)

            all_steps(pool, step)


def kernel(L0_attn_hidden_states, L0_attn_Wq, L0_attn_Wk, L0_attn_Wv, L0_attn_Wo, L0_attn_Wg1, L0_attn_Wg2,
           L0_attn_o_norm_weight, L0_ffn_A, L0_ffn_B, L0_ffn_Wr, L0_ffn_br):
    import ml_dtypes
    import concourse.bacc as bacc
    from concourse.bass_utils import run_bass_kernel_spmd

    def tiled(w):
        return np.ascontiguousarray(w.reshape(KT, P, -1).transpose(1, 0, 2))

    x = np.ascontiguousarray(L0_attn_hidden_states)
    halves = np.arange(D).reshape(2, 16, 2, HH).transpose(0, 2, 1, 3).reshape(-1)
    wqkv = np.stack([tiled(np.asarray(L0_attn_Wq).T[:, halves]), tiled(np.asarray(L0_attn_Wk).T[:, halves]),
                     tiled(np.asarray(L0_attn_Wv).T)])
    wlr = tiled(np.concatenate([np.asarray(L0_attn_Wg1).T, np.asarray(L0_ffn_Wr).T], axis=1))
    bf = ml_dtypes.bfloat16
    pos = np.arange(S, dtype=np.float32)
    inv = (np.float32(1.0) / np.float32(10000.0) ** (np.arange(0, HD, 2, dtype=np.float32) / np.float32(HD))).astype(np.float32)
    ang = pos[None, :] * inv[:, None]
    rope = np.tile(np.stack([np.cos(ang), np.sin(ang)], axis=1), (16, 1, 1)).astype(np.float32)
    krows = (np.arange(NC_)[:, None] == np.arange(S)[None, :] // CH).astype(bf)
    krows[NC_ - 1] = 1
    tok = (np.arange(QT)[None, :] * P + np.arange(P)[:, None]) // CH
    ids = np.arange(NC_)[None, None, :]
    cbias = np.where(ids > tok[:, :, None], NEG, np.where(ids == tok[:, :, None], -NEG, 0.0)).astype(np.float32)
    tri = np.where(np.arange(P)[None, :] > np.arange(P)[:, None], MASK, 0.0).astype(bf)
    sel = np.zeros((P, VW), np.float32)
    for r in range(4):
        sel[32 * r:32 * r + VW] = np.eye(VW)
    hmean = np.kron(np.eye(8), np.full((HD, HD), 1.0 / HD)).astype(np.float32)
    arrays = {
        "x": x, "wqkv": wqkv, "wlr": wlr, "wg2": np.ascontiguousarray(np.asarray(L0_attn_Wg2).T),
        "wo": tiled(np.asarray(L0_attn_Wo).T), "wa": tiled(np.asarray(L0_ffn_A).reshape(NE * RANK, D).T),
        "wb": tiled(np.asarray(L0_ffn_B).transpose(0, 2, 1).reshape(NE * RANK, D)),
        "onorm": np.asarray(L0_attn_o_norm_weight).reshape(HD, 1), "br": np.asarray(L0_ffn_br),
        "rope": rope, "krows": krows, "cbias": cbias, "identf": np.eye(P, dtype=np.float32),
        "identb": np.eye(P).astype(bf), "tri": tri, "sel": sel, "hmean": hmean,
    }
    nc = bacc.Bacc("TRN2", target_bir_lowering=False, num_devices=1)
    args = [nc.dram_tensor(n, a.shape, mybir.dt.from_np(a.dtype), kind="ExternalInput").ap() for n, a in arrays.items()]
    out = nc.dram_tensor("out", x.shape, F32, kind="ExternalOutput").ap()
    nc.disable_value_cache = True
    build(nc, *args, out)
    r = run_bass_kernel_spmd(nc, [arrays], core_ids=[0])
    return r.results[0]["out"]
```
